# Optimizing a Trainium2 kernel written in Bass

```python
import numpy as np
import jax
import jax.numpy as jnp

def _softmax(x, axis=-1):
    return jax.nn.softmax(x, axis=axis)

def _gelu(x):
    return jax.nn.gelu(x, approximate=True)

def _silu(x):
    return jax.nn.silu(x)

def _sigmoid(x):
    return jax.nn.sigmoid(x)

def _layernorm(x, axis=-1, eps=1e-05):
    m = jnp.mean(x, axis=axis, keepdims=True)
    v = jnp.var(x, axis=axis, keepdims=True)
    return (x - m) / jnp.sqrt(v + eps)

def _scatter_add(tgt, idx, src, axis=0):
    return tgt.at[idx].add(src)

def _segment_sum(src, seg, n):
    return jax.ops.segment_sum(src, seg, n)
kernel_name = 'mk_flamingo_gated_d1_seqx_r4_49564b'

def setup_inputs(seed: int=0):
    np.random.seed(seed)
    _w = jnp.asarray

    def _rec_inputs():
        import jax
        import jax.numpy as jnp
        _rk = jax.random.key(seed)
        x = -0.0002928 + 1 * jax.random.normal(jax.random.fold_in(_rk, 1), (16, 256, 256), jnp.float32)
        _lenS = 256 - jax.random.randint(jax.random.fold_in(_rk, 7), (16,), 0, max(1, 256 // 4) + 1, jnp.int32)
        _lenS2 = 256 - jax.random.randint(jax.random.fold_in(_rk, 8), (16,), 0, max(1, 256 // 4) + 1, jnp.int32)
        _ctx_1024P = jax.random.normal(jax.random.fold_in(_rk, 11), (16, 16, 256), jnp.float32)
        _ctx_1024c = jax.random.dirichlet(jax.random.fold_in(_rk, 511), 0.3 * jnp.ones((16,), jnp.float32), (16, 256))
        _ctx_1024t = jnp.einsum('bsk,bkd->bsd', _ctx_1024c, _ctx_1024P)
        _ctx_1024t = _ctx_1024t * jax.lax.rsqrt(jnp.mean(jnp.square(_ctx_1024t)) + 1e-12) * 0.953939
        ctx_1024 = 2.81802e-05 + 1.00001 * (_ctx_1024t + 0.3 * jax.random.normal(jax.random.fold_in(_rk, 611), (16, 256, 256), jnp.float32))
        _validS = jnp.arange(256)[None, :] < _lenS[:, None]
        _validS2 = jnp.arange(256)[None, :] < _lenS2[:, None]
        _causal = jnp.tril(jnp.ones((256, 256), dtype=bool))
        mask_BxS2_bk1 = jnp.broadcast_to(_validS2[:, :], (16, 256))
        _g = jax.random.normal(jax.random.fold_in(_rk, 9001), (2, 1), jnp.float32)
        _g = jnp.sign(_g) * jnp.maximum(jnp.abs(_g), 1.0) + (_g == 0) * 1.0
        g_xattn = _g[0]
        g_ffn = _g[1]
        return (x, ctx_1024, mask_BxS2_bk1, g_xattn, g_ffn)
    x, ctx_1024, mask_BxS2_bk1, g_xattn, g_ffn = _rec_inputs()

    def _L0_xattn_setup():
        import jax, jax.numpy as jnp
        import numpy as np
        B, N, M = (4, 256, 1024)
        DQ, DC = (256, 256)
        H, DH = (16, 64)
        INNER = H * DH
        SCALE = DH ** (-0.5)
        key = jax.random.key(seed)
        ks = jax.random.split(key, 6)
        x = jax.random.normal(ks[0], (B, N, DQ), dtype=jnp.float32)
        context = jax.random.normal(ks[1], (B, M, DC), dtype=jnp.float32)
        mask = jax.random.bernoulli(ks[2], 0.9, (B, M))
        Wq = jax.random.normal(ks[3], (DQ, INNER), dtype=jnp.float32) / np.sqrt(DQ)
        Wkv = jax.random.normal(ks[4], (DC, 2 * INNER), dtype=jnp.float32) / np.sqrt(DC)
        Wo = jax.random.normal(ks[5], (INNER, DQ), dtype=jnp.float32) / np.sqrt(INNER)
        bo = jnp.zeros((DQ,), dtype=jnp.float32)
        return {'x': x, 'context': context, 'mask': mask, 'Wq': Wq, 'Wkv': Wkv, 'Wo': Wo, 'bo': bo}
    _L0_xattn_all = _L0_xattn_setup()
    _L0_xattn_in = {k: v for k, v in _L0_xattn_all.items() if k in ('Wq', 'Wkv', 'Wo', 'bo')}
    del _L0_xattn_all

    def _L0_ffn_setup():
        import jax, jax.numpy as jnp
        import numpy as np
        B, S, D, F, E, R = (4, 512, 256, 1024, 8, 4)
        key = jax.random.key(seed)
        ks = jax.random.split(key, 8)
        s_in = 1.0 / np.sqrt(D)
        s_ff = 1.0 / np.sqrt(F)
        return {'hidden_states': jax.random.normal(ks[0], (B, S, D), jnp.float32), 'gate_W': jax.random.normal(ks[1], (E, D), jnp.float32) * s_in, 'gate_b': jnp.zeros((E,), jnp.float32), 'wi_W': jax.random.normal(ks[2], (F, D), jnp.float32) * s_in, 'wi_b': jnp.zeros((F,), jnp.float32), 'wo_W': jax.random.normal(ks[3], (D, F), jnp.float32) * s_ff, 'wo_b': jnp.zeros((D,), jnp.float32), 'lora_A': jax.random.normal(ks[4], (E, R, D), jnp.float32) * s_in, 'lora_B': jax.random.normal(ks[5], (E, F, R), jnp.float32) * 0.02}
    _L0_ffn_all = _L0_ffn_setup()
    _L0_ffn_in = {k: v for k, v in _L0_ffn_all.items() if k in ('gate_W', 'gate_b', 'wi_W', 'wi_b', 'wo_W', 'wo_b', 'lora_A', 'lora_B')}
    del _L0_ffn_all
    return {'x': x, 'ctx_1024': ctx_1024, 'mask_BxS2_bk1': mask_BxS2_bk1, 'g_xattn': g_xattn, 'g_ffn': g_ffn, 'L0_xattn_Wq': _L0_xattn_in['Wq'], 'L0_xattn_Wkv': _L0_xattn_in['Wkv'], 'L0_xattn_Wo': _L0_xattn_in['Wo'], 'L0_xattn_bo': _L0_xattn_in['bo'], 'L0_ffn_gate_W': _L0_ffn_in['gate_W'], 'L0_ffn_gate_b': _L0_ffn_in['gate_b'], 'L0_ffn_wi_W': _L0_ffn_in['wi_W'], 'L0_ffn_wi_b': _L0_ffn_in['wi_b'], 'L0_ffn_wo_W': _L0_ffn_in['wo_W'], 'L0_ffn_wo_b': _L0_ffn_in['wo_b'], 'L0_ffn_lora_A': _L0_ffn_in['lora_A'], 'L0_ffn_lora_B': _L0_ffn_in['lora_B']}

def reference(x, ctx_1024, mask_BxS2_bk1, g_xattn, g_ffn, L0_xattn_Wq, L0_xattn_Wkv, L0_xattn_Wo, L0_xattn_bo, L0_ffn_gate_W, L0_ffn_gate_b, L0_ffn_wi_W, L0_ffn_wi_b, L0_ffn_wo_W, L0_ffn_wo_b, L0_ffn_lora_A, L0_ffn_lora_B):
    import jax
    import jax.numpy as jnp

    def _L0_xattn_ref(x, context, mask, Wq, Wkv, Wo, bo):
        import jax, jax.numpy as jnp
        import numpy as np
        B, N, M = (4, 256, 1024)
        DQ, DC = (256, 256)
        H, DH = (16, 64)
        INNER = H * DH
        SCALE = DH ** (-0.5)
        q = x @ Wq
        kv = context @ Wkv
        k, v = jnp.split(kv, 2, axis=-1)

        def heads(t):
            b, s, _ = t.shape
            return t.reshape(b, s, H, DH).transpose(0, 2, 1, 3)
        q, k, v = (heads(q), heads(k), heads(v))
        sim = jnp.einsum('bhid,bhjd->bhij', q, k) * SCALE
        max_neg = -jnp.finfo(sim.dtype).max
        sim = jnp.where(mask[:, None, None, :], sim, max_neg)
        sim = jnp.clip(sim, -5.0, 5.0)
        attn = jax.nn.softmax(sim, axis=-1)
        out = jnp.einsum('bhij,bhjd->bhid', attn, v)
        out = out.transpose(0, 2, 1, 3).reshape(x.shape[0], x.shape[1], INNER)
        return out @ Wo + bo

    def _L0_ffn_ref(hidden_states, gate_W, gate_b, wi_W, wi_b, wo_W, wo_b, lora_A, lora_B):
        import jax, jax.numpy as jnp
        import numpy as np
        B, S, D, F, E, R = (4, 512, 256, 1024, 8, 4)
        x = hidden_states
        logits = jnp.einsum('bsd,ed->bse', x, gate_W) + gate_b
        top1 = jnp.argmax(jax.nn.softmax(logits, axis=-1), axis=-1)
        base = jnp.einsum('bsd,fd->bsf', x, wi_W) + wi_b
        out = jnp.zeros_like(x)
        for i in range(lora_A.shape[0]):
            lora = jnp.einsum('bsr,fr->bsf', jnp.einsum('bsd,rd->bsr', x, lora_A[i]), lora_B[i])
            inter = jax.nn.relu(base + lora)
            expert_out = jnp.einsum('bsf,df->bsd', inter, wo_W) + wo_b
            mask = (top1 == i).astype(x.dtype)[..., None]
            out = out + mask * expert_out
        return out
    x = x + jnp.tanh(g_xattn[0]) * _L0_xattn_ref(_layernorm(x, axis=-1), ctx_1024, mask_BxS2_bk1, L0_xattn_Wq, L0_xattn_Wkv, L0_xattn_Wo, L0_xattn_bo)
    x = x + jnp.tanh(g_ffn[0]) * _L0_ffn_ref(_layernorm(x, axis=-1), L0_ffn_gate_W, L0_ffn_gate_b, L0_ffn_wi_W, L0_ffn_wi_b, L0_ffn_wo_W, L0_ffn_wo_b, L0_ffn_lora_A, L0_ffn_lora_B)
    return x

_drawn_inputs = setup_inputs


def setup_inputs(seed=0):
    import zlib

    import numpy as np

    out = dict(_drawn_inputs(seed))
    spreads = {'L0_xattn_bo': (0.0, 0.1),
     'L0_ffn_gate_b': (0.0, 0.8),
     'L0_ffn_wi_b': (0.0, 0.1),
     'L0_ffn_wo_b': (0.0, 0.1)}
    factors = {'L0_ffn_gate_W': 2.953, 'L0_ffn_lora_A': 2.752, 'L0_ffn_lora_B': 2.758}
    for name, (base, spread) in spreads.items():
        noise = np.random.default_rng([zlib.crc32(name.encode()), seed]).standard_normal(out[name].shape)
        drawn = base * np.exp(spread * noise) if base else spread * noise
        out[name] = jnp.asarray(drawn.astype(out[name].dtype))
    for name, factor in factors.items():
        out[name] = (out[name] * factor).astype(out[name].dtype)
    return out
```

```python
import concourse.bass as bass
from concourse import mybir
from contextlib import ExitStack


def gated_cross_attention_and_lora_ffn(nc, x, ctxT, mask, g_xattn, g_ffn, Wq, Wkv, Wo, bo, gateA, gate_b,
                                       wiT, wi_b, woT, wo_b, loraB, out):
    F32, F32R, U8 = mybir.dt.float32, mybir.dt.float32r, mybir.dt.uint8
    ALU, ACT, AX = mybir.AluOpType, mybir.ActivationFunctionType, mybir.AxisListType

    B, T, D = x.shape
    M = ctxT.shape[3]
    INNER = Wq.shape[1]
    DH = 64
    H = INNER // DH
    NP = H // 2
    NG = NP // 2
    KC = D // 128
    JC = M // 128
    IT = T // 128
    F = wiT.shape[1]
    FC = F // 128
    E, ER = gate_b.shape[1], loraB.shape[0]
    R = ER // E
    GA = E + ER
    SCALE = DH ** -0.5
    LO_BOUND, HI_BOUND = 0.006737947, 148.41316
    EPS = 1e-5

    with ExitStack() as ctx:
        def sb(name, shape, dt=F32):
            return ctx.enter_context(nc.sbuf_tensor(name, shape, dt))

        def pair_of(name, shape):
            return sb(name + "_hi", shape, F32R), sb(name + "_lo", shape, F32R)

        wq = pair_of("wq", [128, KC, INNER])
        wk = pair_of("wk", [128, KC, INNER])
        wv = pair_of("wv", [128, KC, INNER])
        wo = pair_of("wo", [128, NP, D])
        wi = pair_of("wi", [128, KC, F])
        wf = pair_of("wf", [128, FC, D])
        lora_w = sb("lora_w", [128, F], F32R)
        gate_w = sb("gate_w", [128, KC, GA])
        stage = sb("stage", [128, 1024])

        ident = sb("ident", [128, 128])
        neg_half = sb("neg_half", [128, IT])
        rank = sb("rank", [128, IT, E])
        lo_rows = sb("lo_rows", [128, 1])
        gates = sb("gates", [128, 2])
        tgate = sb("tgate", [128, 2])
        bo_row = sb("bo_row", [128, D])
        fb_row = sb("fb_row", [128, D])
        gb_row = sb("gb_row", [128, E])
        mask_u8 = sb("mask_u8", [128, B * JC], U8)
        bound = sb("bound", [128, B * JC])
        bound_b = sb("bound_b", [128, 2, JC])

        x_in = sb("x_in", [128, IT, D])
        stats = sb("stats", [128, IT, 6])
        moments = sb("moments", [128, IT, 2])
        var_eps = sb("var_eps", [128, IT])
        rstd = sb("rstd", [128, IT])
        xT = pair_of("xT", [128, KC, T])
        c_in = sb("c_in", [128, KC, M])
        cT = pair_of("cT", [128, KC, M])
        qT = pair_of("qT", [128, 2, 2, T])
        kT = pair_of("kT", [128, 2, 2, M])
        v = sb("v", [128, JC, NP, 3, DH])
        probs = sb("probs", [128, 2, 2, JC, T])
        den = sb("den", [128, 2, T])
        o_raw = sb("o_raw", [128, 4, T])
        oT = pair_of("oT", [128, NP, T])

        x2 = sb("x2", [128, IT, D])
        stats2 = sb("stats2", [128, IT, 6])
        moments2 = sb("moments2", [128, IT, 2])
        var_eps2 = sb("var_eps2", [128, IT])
        rstd2 = sb("rstd2", [128, IT])
        x2n = sb("x2n", [128, IT, D])
        x2T_full = sb("x2T_full", [128, KC, T])
        x2T = pair_of("x2T", [128, KC, T])
        logits = sb("logits", [128, IT, E])
        top = sb("top", [128, IT])
        ranked = sb("ranked", [128, IT, E])
        first = sb("first", [128, IT])
        chosen = sb("chosen", [128, IT, E])
        down = sb("down", [128, IT, ER])
        down_s = sb("down_s", [128, IT, 128], F32R)
        downT = sb("downT", [128, T], F32R)
        inter = pair_of("inter", [128, FC, T])

        s_ps = [ctx.enter_context(nc.psum_tensor(f"s_ps{i}", [128, 2, JC, T], F32)) for i in range(2)]
        o_ps = [ctx.enter_context(nc.psum_tensor(f"o_ps{i}", [128, 2, T], F32)) for i in range(2)]
        g_ps = [ctx.enter_context(nc.psum_tensor(f"g_ps{i}", [128, 512], F32)) for i in range(2)]

        per, sems = {}, {}

        def event(name, n, dma=False):
            sems[name] = ctx.enter_context(nc.semaphore(name))
            per[name] = (n, 16 if dma else 1)
            return sems[name]

        x_loaded = event("x_loaded", 1, True)
        ctx_loaded = event("ctx_loaded", 1, True)
        res_loaded = event("res_loaded", 1, True)
        y_stored = event("y_stored", 1, True)
        q_mm = event("q_mm", NG)
        k_mm = event("k_mm", NG)
        v_mm = event("v_mm", 4)
        xT_mm = event("xT_mm", 1)
        s_mm = event("s_mm", NP)
        pv_mm = event("pv_mm", NP)
        wo_mm = event("wo_mm", IT)
        x2T_mm = event("x2T_mm", 1)
        gate_mm = event("gate_mm", 1)
        downT_mm = event("downT_mm", 1)
        up_mm = event("up_mm", 4)
        y_mm = event("y_mm", IT)
        q_hi = event("q_hi", NG)
        k_hi = event("k_hi", NG)
        v_ready = event("v_ready", 4)
        xT_hi = event("xT_hi", 1)
        ctx_hi = event("ctx_hi", 1)
        exp_done = event("exp_done", NP)
        den_copied = event("den_copied", NP)
        o_hi = event("o_hi", NG)
        x2T_hi = event("x2T_hi", 1)
        downT_ready = event("downT_ready", 1)
        inter_hi = event("inter_hi", 4)
        q_lo = event("q_lo", NG)
        k_lo = event("k_lo", NG)
        bound_set = event("bound_set", 1)
        stats_done = event("stats_done", 2)
        moments_done = event("moments_done", 2)
        var_ready = event("var_ready", 1)
        x_normed = event("x_normed", 1)
        xT_lo = event("xT_lo", 1)
        ctx_lo = event("ctx_lo", 1)
        probs_ready = event("probs_ready", NP)
        den_inv = event("den_inv", NP)
        o_normed = event("o_normed", NP)
        x2_ready = event("x2_ready", IT)
        stats2_done = event("stats2_done", 2)
        moments2_done = event("moments2_done", 2)
        var2_ready = event("var2_ready", 1)
        x2_normed = event("x2_normed", 1)
        x2T_lo = event("x2T_lo", 1)
        pick = event("pick", 8)
        down_ready = event("down_ready", 1)
        inter_lo = event("inter_lo", 4)
        y_ready = event("y_ready", IT)
        rstd_ready = event("rstd_ready", 1)
        rstd2_ready = event("rstd2_ready", 1)
        res_biased = event("res_biased", 1)
        x2_biased = event("x2_biased", 1)
        o_lo = event("o_lo", NG)

        w_loaded = [ctx.enter_context(nc.semaphore(f"w_loaded{i}")) for i in range(2)]
        early_loaded = ctx.enter_context(nc.semaphore("early_loaded"))
        late_loaded = ctx.enter_context(nc.semaphore("late_loaded"))
        small_loaded = ctx.enter_context(nc.semaphore("small_loaded"))
        lora_loaded = ctx.enter_context(nc.semaphore("lora_loaded"))
        w_hi = ctx.enter_context(nc.semaphore("w_hi"))
        w_lo = ctx.enter_context(nc.semaphore("w_lo"))
        pool_const = ctx.enter_context(nc.semaphore("pool_const"))
        dve_const = ctx.enter_context(nc.semaphore("dve_const"))
        act_const = ctx.enter_context(nc.semaphore("act_const"))

        def wait(eng, sem, b, k=0):
            n, unit = per_of(sem)
            value = b * (n * unit) + (k + 1) * unit
            if isinstance(b, int) and value <= 0:
                return
            eng.wait_ge(sem, value)

        def per_of(sem):
            for name, s in sems.items():
                if s is sem:
                    return per[name]
            raise KeyError

        def as_f32(ap):
            return ap.bitcast(F32)

        UNITS = [
            [("k", "b", 1, k_lo), ("v", "b", 2, v_ready)],
            [("q", "b", 2, q_lo), ("wo", "c", 0, x2_ready)],
            [("k", "b", 2, k_lo), ("wo", "c", 1, x2_ready)],
            [("q", "b", 3, q_lo), ("v", "b", 3, v_ready), ("x2T", "c", 0, x2T_hi), ("gate", "c", 0, down_ready)],
            [("k", "b", 3, k_lo), ("downT", "c", 0, downT_ready), ("up", "c", 0, inter_lo),
             ("up", "c", 1, inter_lo), ("xT", "n", 0, xT_lo)],
            [("q", "n", 0, q_lo), ("up", "c", 2, inter_lo), ("up", "c", 3, inter_lo)],
            [("k", "n", 0, k_lo), ("v", "n", 0, v_ready), ("y", "c", 0, y_ready)],
            [("y", "c", 1, y_ready), ("q", "n", 1, q_lo), ("v", "n", 1, v_ready)],
        ]
        bank_of, order = {}, []
        for step in UNITS:
            for u in step:
                bank_of[u[0], u[1], u[2]] = len(order) % 2
                order.append(u)
        assert len(order) % 2 == 0 and len(UNITS) == NP

        def bank(what, who, k):
            return g_ps[bank_of[what, who, k]]

        def who_runs(t):
            if not isinstance(t, int):
                return "bcn"
            return ("b" if 0 <= t < B else "") + ("c" if 0 <= t - 1 < B else "") + ("n" if 0 <= t + 1 < B else "")

        def seq(t, who):
            return {"b": t, "c": t - 1, "n": t + 1}[who]

        def units(t, p):
            return [u for u in UNITS[p] if u[1] in who_runs(t)]

        def wait_bank(pe, t, unit):
            at = order.index(unit)
            here = [u for u in order[:at] if u[1] in who_runs(t) and bank_of[u[:3]] == bank_of[unit[:3]]]
            if here:
                u = here[-1]
                wait(pe, u[3], seq(t, u[1]), u[2])
                return
            if isinstance(t, int) and t <= -1:
                return
            before = who_runs(t - 1)
            u = [u for u in order if u[1] in before and bank_of[u[:3]] == bank_of[unit[:3]]][-1]
            wait(pe, u[3], seq(t - 1, u[1]), u[2])

        EARLY = [wq, wk, wv]
        early_stage = [flat.rearrange("p (k n) -> p k n", k=KC) for flat in
                       (probs[:, :, :, :, :].rearrange("p a h j t -> p (a h j t)"),
                        v[:, :, :, :, :].rearrange("p j a b d -> p (j a b d)")[:, 0:KC * INNER])]
        early_src = [Wq.rearrange("(k p) n -> p k n", p=128), Wkv[:, 0:INNER].rearrange("(k p) n -> p k n", p=128),
                     Wkv[:, INNER:2 * INNER].rearrange("(k p) n -> p k n", p=128)]
        wo_src = Wo.rearrange("(c p) n -> p c n", p=128)
        wi_src = wiT.rearrange("(k p) n -> p k n", p=128)
        wf_src = woT.rearrange("(c p) n -> p c n", p=128)
        LATE = []
        for w, src in ((wo, wo_src), (wi, wi_src), (wf, wf_src)):
            half = w[0].shape[1] // 2
            for i in range(2):
                LATE.append((w, src, slice(i * half, (i + 1) * half), w[0].shape[2]))
        NE = len(EARLY)

        def stage_view(n):
            width = LATE[n][3]
            return stage[:, :].rearrange("p (c n) -> p c n", n=width)

        block = ctx.enter_context(nc.Block())

        @block.sync
        def _(sp):
            def early(n):
                sp.dma_start(early_stage[n % 2], early_src[n]).then_inc(w_loaded[n % 2], 16)

            def load_x(b):
                wait(sp, xT_mm, b, -1)
                sp.dma_start(x_in[:, :, :], x[bass.ds(b, 1), :, :].rearrange("a (i p) d -> p (a i) d", p=128)) \
                    .then_inc(x_loaded, 16)

            def load_ctx(b):
                wait(sp, ctx_lo, b, -1)
                sp.dma_start(c_in[:, :, :], ctxT[bass.ds(b, 1), :, :, :].rearrange("a p k m -> p (a k) m")) \
                    .then_inc(ctx_loaded, 16)

            def load_residual(b):
                wait(sp, y_ready, b, -1)
                sp.dma_start(x2[:, :, :], x[bass.ds(b, 1), :, :].rearrange("a (i p) d -> p (a i) d", p=128)) \
                    .then_inc(res_loaded, 16)

            def store(b):
                wait(sp, y_ready, b, IT - 1)
                sp.dma_start(out[bass.ds(b, 1), :, :].rearrange("a (i p) d -> p (a i) d", p=128), x2n[:, :, :]) \
                    .then_inc(y_stored, 16)

            def iteration(t):
                who = who_runs(t)
                if "n" in who:
                    load_x(seq(t, "n"))
                    load_ctx(seq(t, "n"))
                if "c" in who:
                    store(seq(t, "c"))
                if "b" in who:
                    load_residual(seq(t, "b"))

            load_x(0)
            load_ctx(0)
            early(0)
            early(1)
            sp.dma_start(gates[:, 0:1], g_xattn[0:1, :].to_broadcast([128, 1])).then_inc(small_loaded, 16)
            sp.dma_start(gates[:, 1:2], g_ffn[0:1, :].to_broadcast([128, 1])).then_inc(small_loaded, 16)
            sp.dma_start(mask_u8[:, :], mask).then_inc(small_loaded, 16)
            sp.dma_start(bo_row[:, :], bo[0:1, :].to_broadcast([128, D])).then_inc(small_loaded, 16)
            sp.dma_start(fb_row[:, :], wo_b[0:1, :].to_broadcast([128, D])).then_inc(small_loaded, 16)
            sp.dma_start(gb_row[:, :], gate_b[0:1, :].to_broadcast([128, E])).then_inc(small_loaded, 16)
            sp.dma_start(gate_w[:, :, :], gateA.rearrange("(k p) n -> p k n", p=128)).then_inc(small_loaded, 16)
            sp.wait_ge(w_lo, 1)
            early(2)
            sp.wait_ge(pool_const, 1)
            for q in range(3):
                sp.dma_start(stage[ER * q:ER * q + ER, :], loraB).then_inc(lora_loaded, 16)
            sp.dma_start(stage[96:98, :], wi_b[0:1, :].to_broadcast([2, F])).then_inc(lora_loaded, 16)
            load_x(1)
            load_ctx(1)
            for n in range(len(LATE)):
                _, src, part, _ = LATE[n]
                sp.wait_ge(w_lo, NE + 1 + n)
                sp.dma_start(stage_view(n), src[:, part, :]).then_inc(late_loaded, 16)
            load_residual(0)
            iteration(1)
            with sp.Fori(2, B - 1) as t:
                iteration(t)
            iteration(B - 1)
            iteration(B)
            wait(sp, y_stored, B - 1)

        @block.gpsimd
        def _(pool):
            pool.memset(stage[:, :], 0.0).then_inc(pool_const, 1)
            pool.memset(ident[:, :], 0.0).then_inc(pool_const, 1)
            pool.memset(lo_rows[:, :], 0.0).then_inc(pool_const, 1)
            pool.memset(neg_half[:, :], -0.5).then_inc(pool_const, 1)
            for e in range(E):
                last = pool.memset(rank[:, :, e:e + 1], float(E - e))
            last.then_inc(pool_const, 1)
            pool.wait_ge(pool_const, 5)
            pool.affine_select(out=ident[:, :], in_=ident[:, :], compare_op=ALU.not_equal, fill=1.0,
                               base=0, pattern=[[-1, 128]], channel_multiplier=1).then_inc(pool_const, 1)
            pool.wait_ge(pool_const, 6)
            pool.memset(lo_rows[2 * ER:3 * ER, :], -1.0).then_inc(pool_const, 1)
            pool.wait_ge(pool_const, 7)
            pool.affine_select(out=lo_rows[:, :], in_=lo_rows[:, :], compare_op=ALU.not_equal, fill=-1.0,
                               base=-97, pattern=[[0, 1]], channel_multiplier=1).then_inc(pool_const, 1)

            def rstd_of(out_, var, ready, done, b):
                wait(pool, ready, b)
                pool.tensor_tensor(out_[:, :], var[:, :], neg_half[:, :], ALU.pow).then_inc(done, 1)

            def split_o(b, g):
                wait(pool, wo_mm, b, -1)
                wait(pool, o_hi, b, g)
                s = 2 * (g % 2)
                pool.tensor_tensor(oT[1][:, 2 * g:2 * g + 2, :], o_raw[:, s:s + 2, :],
                                   as_f32(oT[0][:, 2 * g:2 * g + 2, :]), ALU.subtract).then_inc(o_lo, 1)

            def iteration(t):
                who = who_runs(t)
                b, c, n = (seq(t, w) for w in "bcn")
                if "c" in who:
                    split_o(c, NG - 1)
                    wait(pool, res_loaded, c)
                    pool.tensor_tensor(x2[:, :, :], x2[:, :, :],
                                       bo_row[:, None, :].to_broadcast([128, IT, D]), ALU.add).then_inc(res_biased, 1)
                if "n" in who:
                    rstd_of(rstd, var_eps, var_ready, rstd_ready, n)
                if "c" in who:
                    rstd_of(rstd2, var_eps2, var2_ready, rstd2_ready, c)
                if "b" in who:
                    split_o(b, 0)
                if "c" in who:
                    wait(pool, x2_normed, c)
                    pool.tensor_tensor(x2[:, :, :], x2[:, :, :],
                                       fb_row[:, None, :].to_broadcast([128, IT, D]), ALU.add).then_inc(x2_biased, 1)
                if "b" in who:
                    split_o(b, 1)
                    split_o(b, 2)

            pool.wait_ge(dve_const, 4)
            iteration(-1)
            iteration(0)
            iteration(1)
            with pool.Fori(2, B - 1) as t:
                iteration(t)
            iteration(B - 1)
            iteration(B)

        @block.scalar
        def _(act):
            def evac(out_, in_, done, func=ACT.Copy):
                act.activation(out_, in_, func).then_inc(done, 1)

            def exps(b, p):
                wait(act, s_mm, b, p)
                wait(act, pv_mm, b, p - 2)
                act.activation(probs[:, p % 2, :, :, :], s_ps[p % 2][:, :, :, :], ACT.Exp, scale=SCALE) \
                    .then_inc(exp_done, 1)

            def copy_den(b, p):
                wait(act, pv_mm, b, p)
                wait(act, o_normed, b, p - 2)
                act.activation(den[0:64, p % 2, :], o_ps[p % 2][64:128, 0, :], ACT.Copy)
                act.activation(den[64:128, p % 2, :], o_ps[p % 2][0:64, 1, :], ACT.Copy).then_inc(den_copied, 1)

            def split_o(b, g):
                wait(act, wo_mm, b, -1)
                wait(act, o_normed, b, 2 * g + 1)
                s = 2 * (g % 2)
                evac(oT[0][:, 2 * g:2 * g + 2, :], o_raw[:, s:s + 2, :], o_hi)

            def unit(t, u):
                what, who, k, _ = u
                s = seq(t, who)
                src = bank(what, who, k)[:, :]
                if what == "q":
                    wait(act, q_mm, s, k)
                    wait(act, s_mm, s, 2 * k - 3)
                    evac(qT[0][:, k % 2, :, :], src.rearrange("p (a t) -> p a t", a=2), q_hi)
                elif what == "k":
                    wait(act, k_mm, s, k)
                    wait(act, s_mm, s, 2 * k - 3)
                    evac(kT[0][:, k % 2, :, :], src.rearrange("p (a t) -> p a t", a=2), k_hi)
                elif what == "v":
                    half, j = divmod(k, 2)
                    wait(act, v_mm, s, k)
                    wait(act, pv_mm, s, NP // 2 * (half + 1) - 1 - NP)
                    evac(v[:, j, 4 * half:4 * half + 4, 0:3:2, :],
                         src.rearrange("p (a b d) -> p a b d", b=2, d=DH), v_ready)
                elif what == "xT":
                    wait(act, xT_mm, s)
                    wait(act, q_mm, s, -1)
                    evac(xT[0][:, :, :], src.rearrange("p (k t) -> p k t", k=KC), xT_hi)
                elif what == "x2T":
                    wait(act, x2T_mm, s)
                    act.activation(x2T_full[:, :, :], src.rearrange("p (k t) -> p k t", k=KC), ACT.Copy)
                    evac(x2T[0][:, :, :], src.rearrange("p (k t) -> p k t", k=KC), x2T_hi)
                elif what == "downT":
                    wait(act, downT_mm, s)
                    evac(downT[:, :], src[:, 0:T], downT_ready)
                elif what == "up":
                    wait(act, up_mm, s, k)
                    wait(act, y_mm, s, -1)
                    evac(inter[0][:, 2 * k:2 * k + 2, :], src.rearrange("p (f t) -> p f t", f=2), inter_hi, ACT.Relu)

            def split_ctx(b):
                wait(act, ctx_loaded, b)
                wait(act, k_mm, b, -1)
                wait(act, v_mm, b, -1)
                evac(cT[0][:, :, :], c_in[:, :, :], ctx_hi)

            def late_weight(n):
                act.wait_ge(late_loaded, 16 * (n + 1))
                w, _, part, _ = LATE[n]
                evac(w[0][:, part, :], stage_view(n), w_hi)

            def iteration(t):
                who = who_runs(t)
                b, c, n = (seq(t, w) for w in "bcn")
                for p in range(NP):
                    if p + 1 < NP:
                        if "b" in who:
                            exps(b, p + 1)
                    elif "n" in who:
                        exps(n, 0)
                    if p == 0 and "c" in who:
                        split_o(c, NG - 1)
                    for u in units(t, p):
                        unit(t, u)
                    if p == 4 and "n" in who:
                        split_ctx(n)
                    if "b" in who:
                        copy_den(b, p)
                        if p in (3, 4, 6):
                            split_o(b, {3: 0, 4: 1, 6: 2}[p])
                    if isinstance(t, int) and t == 0 and p < len(LATE):
                        late_weight(p)

            act.wait_ge(small_loaded, 16 * 7)
            act.activation(tgate[:, :], gates[:, :], ACT.Tanh).then_inc(act_const, 1)
            for i in range(NE):
                act.wait_ge(w_loaded[i % 2], 16 * (i // 2 + 1))
                evac(EARLY[i][0][:, :, :], early_stage[i % 2], w_hi)
            act.wait_ge(lora_loaded, 16 * 4)
            evac(lora_w[:, :], stage[:, :], w_hi)
            iteration(-1)
            iteration(0)
            iteration(1)
            with act.Fori(2, B - 1) as t:
                iteration(t)
            iteration(B - 1)
            iteration(B)

        @block.tensor
        def _(pe):
            def three(out_, lhs, rhs, cut_l, cut_r, start, stop):
                pe.matmul(out_, cut_l(lhs[0]), cut_r(rhs[0]), start=start, stop=False)
                pe.matmul(out_, cut_l(lhs[0]), cut_r(rhs[1]), start=False, stop=False)
                return pe.matmul(out_, cut_l(lhs[1]), cut_r(rhs[0]), start=False, stop=stop)

            def scores(b, p):
                wait(pe, exp_done, b, p - 2)
                wait(pe, q_lo, b, p // 2)
                wait(pe, k_lo, b, p // 2)
                slot, a = p // 2 % 2, p % 2
                ps = s_ps[p % 2]
                for j in range(JC):
                    for part, (l, r) in enumerate(((0, 0), (0, 1), (1, 0))):
                        for h in range(2):
                            rows = slice(64 * h, 64 * h + 64)
                            last = pe.matmul(ps[:, h, j, :], kT[l][rows, slot, a, 128 * j:128 * j + 128],
                                             qT[r][rows, slot, a, :], start=(part == 0), stop=(part == 2))
                last.then_inc(s_mm, 1)

            def apply(b, p):
                wait(pe, probs_ready, b, p)
                wait(pe, o_normed, b, p - 2)
                wait(pe, v_ready, b, 1 + 2 * (p // (NP // 2)))
                for h2 in range(2):
                    for j in range(JC):
                        blocks = v[:, j, p, h2:h2 + 2, :].rearrange("k a d -> k (a d)")
                        last = pe.matmul(o_ps[p % 2][:, h2, :], blocks, probs[:, p % 2, h2, j, :],
                                         start=(j == 0), stop=(j == JC - 1))
                last.then_inc(pv_mm, 1)

            def unit(t, u):
                what, who, k, _ = u
                s = seq(t, who)
                ps = bank(what, who, k)
                wait_bank(pe, t, u)
                if what == "q":
                    wait(pe, xT_lo, s)
                    for a in range(2):
                        cols = slice(128 * (2 * k + a), 128 * (2 * k + a) + 128)
                        for c in range(KC):
                            last = three(ps[:, T * a:T * a + T], wq, xT, lambda w: w[:, c, cols],
                                         lambda w: w[:, c, :], c == 0, c == KC - 1)
                    last.then_inc(q_mm, 1)
                elif what == "k":
                    wait(pe, ctx_lo, s)
                    for a in range(2):
                        cols = slice(128 * (2 * k + a), 128 * (2 * k + a) + 128)
                        for c in range(KC):
                            last = three(ps[:, M * a:M * a + M], wk, cT, lambda w: w[:, c, cols],
                                         lambda w: w[:, c, :], c == 0, c == KC - 1)
                    last.then_inc(k_mm, 1)
                elif what == "v":
                    half, j = divmod(k, 2)
                    wait(pe, ctx_lo, s)
                    for c in range(KC):
                        last = three(ps[:, :], cT, wv, lambda w: w[:, c, 128 * j:128 * j + 128],
                                     lambda w: w[:, c, 512 * half:512 * half + 512], c == 0, c == KC - 1)
                    last.then_inc(v_mm, 1)
                elif what == "xT":
                    wait(pe, x_normed, s)
                    for c in range(KC):
                        for i in range(IT):
                            last = pe.transpose(ps[:, T * c + 128 * i:T * c + 128 * i + 128],
                                                x_in[:, i, 128 * c:128 * c + 128], ident[:, :])
                    last.then_inc(xT_mm, 1)
                elif what == "wo":
                    wait(pe, o_lo, s, NG - 1)
                    for c in range(NP):
                        last = three(ps[:, 0:D], oT, wo, lambda w: w[:, c, 128 * k:128 * k + 128],
                                     lambda w: w[:, c, :], c == 0, c == NP - 1)
                    last.then_inc(wo_mm, 1)
                elif what == "x2T":
                    wait(pe, x2_normed, s)
                    for c in range(KC):
                        for i in range(IT):
                            last = pe.transpose(ps[:, T * c + 128 * i:T * c + 128 * i + 128],
                                                x2n[:, i, 128 * c:128 * c + 128], ident[:, :])
                    last.then_inc(x2T_mm, 1)
                elif what == "gate":
                    wait(pe, x2T_hi, s)
                    for i in range(IT):
                        for c in range(KC):
                            last = pe.matmul(ps[:, 64 * i:64 * i + GA], x2T_full[:, c, 128 * i:128 * i + 128],
                                             gate_w[:, c, :], start=(c == 0), stop=(c == KC - 1))
                    last.then_inc(gate_mm, 1)
                elif what == "downT":
                    wait(pe, down_ready, s)
                    for i in range(IT):
                        last = pe.transpose(ps[:, 128 * i:128 * i + 128], as_f32(down_s[:, i, :]), ident[:, :])
                    last.then_inc(downT_mm, 1)
                elif what == "up":
                    wait(pe, x2T_lo, s)
                    wait(pe, downT_ready, s)
                    for a in range(2):
                        cols = slice(128 * (2 * k + a), 128 * (2 * k + a) + 128)
                        o = ps[:, T * a:T * a + T]
                        pe.matmul(o, lora_w[:, cols], downT[:, :], start=True, stop=False)
                        for c in range(KC):
                            last = three(o, wi, x2T, lambda w: w[:, c, cols], lambda w: w[:, c, :],
                                         False, c == KC - 1)
                    last.then_inc(up_mm, 1)
                elif what == "y":
                    wait(pe, inter_lo, s, 3)
                    for f in range(FC):
                        last = three(ps[:, 0:D], inter, wf, lambda w: w[:, f, 128 * k:128 * k + 128],
                                     lambda w: w[:, f, :], f == 0, f == FC - 1)
                    last.then_inc(y_mm, 1)

            def iteration(t):
                who = who_runs(t)
                b, c, n = (seq(t, w) for w in "bcn")
                for p in range(NP):
                    if p + 1 < NP:
                        if "b" in who:
                            scores(b, p + 1)
                    elif "n" in who:
                        scores(n, 0)
                    for u in units(t, p):
                        unit(t, u)
                    if "b" in who:
                        apply(b, p)

            pe.wait_ge(pool_const, 6)
            pe.wait_ge(w_lo, NE)
            pe.wait_ge(dve_const, 5)
            iteration(-1)
            iteration(0)
            pe.wait_ge(w_lo, NE + 1 + len(LATE))
            iteration(1)
            with pe.Fori(2, B - 1) as t:
                iteration(t)
            iteration(B - 1)
            iteration(B)

        @block.vector
        def _(dve):
            def sub(out_, in_, hi, done):
                dve.tensor_tensor(out_, in_, as_f32(hi), ALU.subtract).then_inc(done, 1)

            def clip(b, p):
                wait(dve, exp_done, b, p)
                wait(dve, bound_set, b)
                for j in range(JC):
                    pr = probs[:, p % 2, :, j, :]
                    last = dve.tensor_scalar(pr, pr, bound_b[:, 0, j:j + 1], LO_BOUND, ALU.min, ALU.max)
                last.then_inc(probs_ready, 1)

            def norm_o(b, p):
                wait(dve, den_copied, b, p)
                dve.reciprocal(den[:, p % 2, :], den[:, p % 2, :]).then_inc(den_inv, 1)
                wait(dve, den_inv, b, p)
                g = p // 2
                wait(dve, o_lo, b, g - 2)
                slot = 2 * (g % 2) + p % 2
                dve.tensor_tensor(o_raw[0:64, slot, :], o_ps[p % 2][0:64, 0, :], den[0:64, p % 2, :], ALU.mult)
                dve.tensor_tensor(o_raw[64:128, slot, :], o_ps[p % 2][64:128, 1, :], den[64:128, p % 2, :],
                                  ALU.mult).then_inc(o_normed, 1)

            def layer_stats(src, st, mo, ve, done, mdone, ready, b):
                for i in range(IT):
                    dve.bn_stats(st[:, i, :], src[:, i, :]).then_inc(done, 1)
                wait(dve, done, b, IT - 1)
                dve.tensor_copy(ve[:, 0:1], st[:, IT - 1, 0:1])
                for i in range(IT):
                    dve.bn_aggr(mo[:, i, :], st[:, i, :]).then_inc(mdone, 1)
                wait(dve, mdone, b, IT - 1)
                dve.tensor_scalar(ve[:, :], mo[:, :, 1], EPS, None, ALU.add).then_inc(ready, 1)

            def normalise(dst, src, mo, rs, ready, done, b):
                wait(dve, ready, b)
                for i in range(IT):
                    last = dve.tensor_scalar(dst[:, i, :], src[:, i, :], mo[:, i, 0:1], rs[:, i:i + 1],
                                             ALU.subtract, ALU.mult)
                last.then_inc(done, 1)

            def choose(b, ps):
                g = ps[:, 0:128].rearrange("p (i n) -> p i n", i=IT)
                wait(dve, gate_mm, b)
                dve.tensor_tensor(logits[:, :, :], g[:, :, 0:E], gb_row[:, None, :].to_broadcast([128, IT, E]),
                                  ALU.add).then_inc(pick, 1)
                wait(dve, pick, b, 0)
                dve.tensor_reduce(top[:, :], logits[:, :, :], AX.X, ALU.max).then_inc(pick, 1)
                wait(dve, pick, b, 1)
                dve.tensor_tensor(ranked[:, :, :], logits[:, :, :], top[:, :, None].to_broadcast([128, IT, E]),
                                  ALU.is_equal).then_inc(pick, 1)
                wait(dve, pick, b, 2)
                dve.tensor_tensor(ranked[:, :, :], ranked[:, :, :], rank[:, :, :], ALU.mult).then_inc(pick, 1)
                wait(dve, pick, b, 3)
                dve.tensor_reduce(first[:, :], ranked[:, :, :], AX.X, ALU.max).then_inc(pick, 1)
                wait(dve, pick, b, 4)
                dve.tensor_tensor(chosen[:, :, :], ranked[:, :, :], first[:, :, None].to_broadcast([128, IT, E]),
                                  ALU.is_equal).then_inc(pick, 1)
                wait(dve, pick, b, 5)
                for i in range(IT):
                    last = dve.tensor_tensor(down[:, i, :].rearrange("p (e r) -> p e r", r=R),
                                             g[:, i, E:GA].rearrange("p (e r) -> p e r", r=R),
                                             chosen[:, i, :, None].to_broadcast([128, E, R]), ALU.mult)
                last.then_inc(pick, 1)
                wait(dve, pick, b, 6)
                wait(dve, downT_mm, b, -1)
                dve.tensor_copy(down_s[:, :, 2 * ER:3 * ER], down[:, :, :])
                dve.tensor_copy(down_s[:, :, 0:ER], down[:, :, :]).then_inc(pick, 1)
                wait(dve, pick, b, 7)
                sub(down_s[:, :, ER:2 * ER], down[:, :, :], down_s[:, :, 0:ER], down_ready)

            def unit(t, u):
                what, who, k, _ = u
                s = seq(t, who)
                src = bank(what, who, k)[:, :]
                two = src.rearrange("p (a t) -> p a t", a=2)
                if what == "q":
                    wait(dve, q_hi, s, k)
                    sub(qT[1][:, k % 2, :, :], two, qT[0][:, k % 2, :, :], q_lo)
                elif what == "k":
                    wait(dve, k_hi, s, k)
                    sub(kT[1][:, k % 2, :, :], two, kT[0][:, k % 2, :, :], k_lo)
                elif what == "xT":
                    wait(dve, xT_hi, s)
                    sub(xT[1][:, :, :], two, xT[0][:, :, :], xT_lo)
                elif what == "wo":
                    wait(dve, wo_mm, s, k)
                    wait(dve, res_biased, s)
                    dve.scalar_tensor_tensor(x2[:, k, :], src[:, 0:D], tgate[:, 0:1], x2[:, k, :],
                                             ALU.mult, ALU.add).then_inc(x2_ready, 1)
                    if k == IT - 1:
                        wait(dve, x2_ready, s, k)
                        layer_stats(x2, stats2, moments2, var_eps2, stats2_done, moments2_done, var2_ready, s)
                elif what == "x2T":
                    wait(dve, x2T_hi, s)
                    sub(x2T[1][:, :, :], x2T_full[:, :, :], x2T[0][:, :, :], x2T_lo)
                elif what == "gate":
                    choose(s, src)
                elif what == "up":
                    wait(dve, inter_hi, s, k)
                    dve.scalar_tensor_tensor(inter[1][:, 2 * k:2 * k + 2, :], two, 0.0,
                                             as_f32(inter[0][:, 2 * k:2 * k + 2, :]), ALU.max,
                                             ALU.subtract).then_inc(inter_lo, 1)
                elif what == "y":
                    wait(dve, y_mm, s, k)
                    wait(dve, x2_biased, s)
                    dve.scalar_tensor_tensor(x2n[:, k, :], src[:, 0:D], tgate[:, 1:2], x2[:, k, :],
                                             ALU.mult, ALU.add).then_inc(y_ready, 1)

            def split_ctx(b):
                wait(dve, ctx_hi, b)
                sub(cT[1][:, :, :], c_in[:, :, :], cT[0][:, :, :], ctx_lo)

            def late_weight(n):
                dve.wait_ge(w_hi, NE + 2 + n)
                w, _, part, _ = LATE[n]
                sub(w[1][:, part, :], stage_view(n), w[0][:, part, :], w_lo)

            def iteration(t):
                who = who_runs(t)
                b, c, n = (seq(t, w) for w in "bcn")
                for p in range(NP):
                    if p == NP - 1 and "n" in who:
                        wait(dve, probs_ready, n, -1)
                        dve.tensor_copy(bound_b[:, 0, :], bound[:, bass.ds(n * JC, JC)]).then_inc(bound_set, 1)
                    if p + 1 < NP:
                        if "b" in who:
                            clip(b, p + 1)
                    elif "n" in who:
                        clip(n, 0)
                    if p == 1 and "n" in who:
                        wait(dve, x_loaded, n)
                        layer_stats(x_in, stats, moments, var_eps, stats_done, moments_done, var_ready, n)
                    if p == 3 and "c" in who:
                        wait(dve, y_stored, c, -1)
                        normalise(x2n, x2, moments2, rstd2, rstd2_ready, x2_normed, c)
                    if p == 3 and "n" in who:
                        normalise(x_in, x_in, moments, rstd, rstd_ready, x_normed, n)
                    for u in units(t, p):
                        unit(t, u)
                    if p == 4 and "n" in who:
                        split_ctx(n)
                    if "b" in who:
                        norm_o(b, p)
                    if isinstance(t, int) and t == 0 and p < len(LATE):
                        late_weight(p)

            dve.wait_ge(small_loaded, 16 * 7)
            dve.tensor_scalar(bound[:, :], mask_u8[:, :], HI_BOUND - LO_BOUND, LO_BOUND, ALU.mult, ALU.add) \
                .then_inc(dve_const, 1)
            dve.memset(as_f32(down_s[:, :, 96:98]), 1.0)
            dve.memset(as_f32(down_s[:, :, 98:128]), 0.0).then_inc(dve_const, 1)
            dve.wait_ge(act_const, 1)
            dve.tensor_scalar(bo_row[:, :], bo_row[:, :], tgate[:, 0:1], None, ALU.mult).then_inc(dve_const, 1)
            dve.tensor_scalar(fb_row[:, :], fb_row[:, :], tgate[:, 1:2], None, ALU.mult).then_inc(dve_const, 1)
            for i in range(NE):
                dve.wait_ge(w_hi, i + 1)
                sub(EARLY[i][1][:, :, :], early_stage[i % 2], EARLY[i][0][:, :, :], w_lo)
            dve.wait_ge(w_lo, 2)
            dve.memset(v[:, :, :, 1, :], 1.0).then_inc(dve_const, 1)
            dve.wait_ge(w_hi, NE + 1)
            dve.wait_ge(pool_const, 8)
            dve.scalar_tensor_tensor(lora_w[:, :], as_f32(lora_w[:, :]), lo_rows[:, 0:1], stage[:, :],
                                     ALU.mult, ALU.add).then_inc(w_lo, 1)
            iteration(-1)
            iteration(0)
            iteration(1)
            with dve.Fori(2, B - 1) as t:
                iteration(t)
            iteration(B - 1)
            iteration(B)


def kernel(**inputs):
    import numpy as _np
    import concourse.bacc as _bacc
    from concourse import mybir as _mybir
    from concourse.bass_utils import run_bass_kernel_spmd as _run

    a = {k: _np.asarray(v) for k, v in inputs.items()}
    B, M, D = a["ctx_1024"].shape
    E, R, _ = a["L0_ffn_lora_A"].shape
    F = a["L0_ffn_wi_W"].shape[0]
    feeds = {
        "x": a["x"],
        "ctxT": a["ctx_1024"].reshape(B, M, D // 128, 128).transpose(0, 3, 2, 1),
        "mask": a["mask_BxS2_bk1"].reshape(B, M // 128, 128).transpose(2, 0, 1).reshape(128, -1),
        "g_xattn": a["g_xattn"].reshape(1, 1),
        "g_ffn": a["g_ffn"].reshape(1, 1),
        "Wq": a["L0_xattn_Wq"],
        "Wkv": a["L0_xattn_Wkv"],
        "Wo": a["L0_xattn_Wo"],
        "bo": a["L0_xattn_bo"].reshape(1, -1),
        "gateA": _np.concatenate([a["L0_ffn_gate_W"].T, a["L0_ffn_lora_A"].reshape(E * R, D).T], axis=1),
        "gate_b": a["L0_ffn_gate_b"].reshape(1, -1),
        "wiT": a["L0_ffn_wi_W"].T,
        "wi_b": a["L0_ffn_wi_b"].reshape(1, -1),
        "woT": a["L0_ffn_wo_W"].T,
        "wo_b": a["L0_ffn_wo_b"].reshape(1, -1),
        "loraB": a["L0_ffn_lora_B"].transpose(0, 2, 1).reshape(E * R, F),
    }
    nc = _bacc.Bacc("TRN2", target_bir_lowering=False, num_devices=1)
    arrays, args = {}, []
    for name, value in feeds.items():
        value = _np.ascontiguousarray(value)
        arrays[f"in_{name}"] = value
        args.append(nc.dram_tensor(f"in_{name}", value.shape, _mybir.dt.from_np(value.dtype),
                                   kind="ExternalInput").ap())
    out = nc.dram_tensor("out_y", a["x"].shape, _mybir.dt.float32, kind="ExternalOutput").ap()
    gated_cross_attention_and_lora_ffn(nc, *args, out)
    r = _run(nc, [arrays], core_ids=[0])
    return r.results[0]["out_y"]
```

```python
import concourse.bass as bass
from concourse import mybir
from contextlib import ExitStack


def gated_cross_attention_and_lora_ffn(nc, x, ctxT, mask, g_xattn, g_ffn, Wq, Wkv, Wo, bo, gateA, gate_b,
                                       wiT, wi_b, woT, wo_b, loraB, out):
    F32, F32R, U8 = mybir.dt.float32, mybir.dt.float32r, mybir.dt.uint8
    ALU, ACT, AX = mybir.AluOpType, mybir.ActivationFunctionType, mybir.AxisListType

    B, T, D = x.shape
    M = ctxT.shape[3]
    INNER = Wq.shape[1]
    DH = 64
    H = INNER // DH
    NP = H // 2
    NG = NP // 2
    KC = D // 128
    JC = M // 128
    IT = T // 128
    F = wiT.shape[1]
    FC = F // 128
    E, ER = gate_b.shape[1], loraB.shape[0]
    R = ER // E
    GA = E + ER
    SCALE = DH ** -0.5
    LO_BOUND, HI_BOUND = 0.006737947, 148.41316
    EPS = 1e-5

    with ExitStack() as ctx:
        def sb(name, shape, dt=F32):
            return ctx.enter_context(nc.sbuf_tensor(name, shape, dt))

        def pair_of(name, shape):
            return sb(name + "_hi", shape, F32R), sb(name + "_lo", shape, F32R)

        wq = pair_of("wq", [128, KC, INNER])
        wk = pair_of("wk", [128, KC, INNER])
        wv = pair_of("wv", [128, KC, INNER])
        wo = pair_of("wo", [128, NP, D])
        wi = pair_of("wi", [128, KC, F])
        wf = pair_of("wf", [128, FC, D])
        lora_w = sb("lora_w", [128, F], F32R)
        gate_w = sb("gate_w", [128, KC, GA])

        ident = sb("ident", [128, 128])
        neg_half = sb("neg_half", [128, IT])
        rank = sb("rank", [128, IT, E])
        lo_rows = sb("lo_rows", [128, 1])
        gates = sb("gates", [128, 2])
        tgate = sb("tgate", [128, 2])
        bo_row = sb("bo_row", [128, D])
        fb_row = sb("fb_row", [128, D])
        gb_row = sb("gb_row", [128, E])
        mask_u8 = sb("mask_u8", [128, B * JC], U8)
        bound = sb("bound", [128, B * JC])
        bound_b = sb("bound_b", [128, 2, JC])

        x_in = sb("x_in", [128, IT, D])
        stats = sb("stats", [128, IT, 6])
        moments = sb("moments", [128, IT, 2])
        var_eps = sb("var_eps", [128, IT])
        rstd = sb("rstd", [128, IT])
        xT = pair_of("xT", [128, KC, T])
        c_in = sb("c_in", [128, KC, M])
        cT = pair_of("cT", [128, KC, M])
        qT = pair_of("qT", [128, 2, 2, T])
        kT = pair_of("kT", [128, 2, 2, M])
        v = pair_of("v", [128, JC, NP, 3, DH])
        exp_s = sb("exp_s", [128, 2, JC, T])
        probs = pair_of("probs", [128, 2, 2, JC, T])
        den_T = sb("den_T", [128, T])
        den_inv = sb("den_inv", [128, T // 32])
        o_raw = sb("o_raw", [128, 4, T])
        oT = pair_of("oT", [128, NP, T])

        x2 = sb("x2", [128, IT, D])
        stats2 = sb("stats2", [128, IT, 6])
        moments2 = sb("moments2", [128, IT, 2])
        var_eps2 = sb("var_eps2", [128, IT])
        rstd2 = sb("rstd2", [128, IT])
        x2n = sb("x2n", [128, IT, D])
        x2T_full = x2n[:, :, :]
        x2T = pair_of("x2T", [128, KC, T])
        logits = sb("logits", [128, IT, E])
        top = sb("top", [128, IT])
        ranked = sb("ranked", [128, IT, E])
        first = sb("first", [128, IT])
        chosen = sb("chosen", [128, IT, E])
        down = sb("down", [128, IT, ER])
        down_s = sb("down_s", [128, IT, 128], F32R)
        downT = sb("downT", [128, T], F32R)
        inter = pair_of("inter", [128, FC, T])

        s_ps = [ctx.enter_context(nc.psum_tensor(f"s_ps{i}", [128, 2, JC, T], F32)) for i in range(2)]
        o_ps = [ctx.enter_context(nc.psum_tensor(f"o_ps{i}", [128, 2, T], F32)) for i in range(2)]
        g_ps = [ctx.enter_context(nc.psum_tensor(f"g_ps{i}", [128, 512], F32)) for i in range(2)]

        per, sems = {}, {}

        def event(name, n, dma=False):
            sems[name] = ctx.enter_context(nc.semaphore(name))
            per[name] = (n, 16 if dma else 1)
            return sems[name]

        x_loaded = event("x_loaded", 1, True)
        ctx_loaded = event("ctx_loaded", 1, True)
        res_loaded = event("res_loaded", 1, True)
        y_stored = event("y_stored", 1, True)
        q_mm = event("q_mm", NG)
        k_mm = event("k_mm", NG)
        v_mm = event("v_mm", 4)
        xT_mm = event("xT_mm", 1)
        s_mm = event("s_mm", NP)
        pv_mm = event("pv_mm", NP)
        wo_mm = event("wo_mm", IT)
        x2T_mm = event("x2T_mm", 1)
        gate_mm = event("gate_mm", 1)
        downT_mm = event("downT_mm", 1)
        up_mm = event("up_mm", 4)
        y_mm = event("y_mm", IT)
        q_hi = event("q_hi", NG)
        k_hi = event("k_hi", NG)
        v_hi = event("v_hi", 4)
        xT_hi = event("xT_hi", 1)
        ctx_hi = event("ctx_hi", 1)
        exp_done = event("exp_done", NP)
        probs_hi = event("probs_hi", NP)
        den_copied = event("den_copied", NP)
        o_hi = event("o_hi", NG)
        x2T_hi = event("x2T_hi", 1)
        downT_ready = event("downT_ready", 1)
        inter_hi = event("inter_hi", 4)
        q_lo = event("q_lo", NG)
        k_lo = event("k_lo", NG)
        bound_set = event("bound_set", 1)
        stats_done = event("stats_done", 2)
        moments_done = event("moments_done", 2)
        var_ready = event("var_ready", 1)
        x_normed = event("x_normed", 1)
        xT_lo = event("xT_lo", 1)
        ctx_lo = event("ctx_lo", 1)
        v_lo = event("v_lo", 4)
        clipped = event("clipped", NP)
        probs_lo = event("probs_lo", NP)
        den_turned = event("den_turned", NP)
        inverted = event("inverted", NP)
        inv_spread = event("inv_spread", NP)
        o_normed = event("o_normed", NP)
        x2_ready = event("x2_ready", IT)
        stats2_done = event("stats2_done", 2)
        moments2_done = event("moments2_done", 2)
        var2_ready = event("var2_ready", 1)
        x2_normed = event("x2_normed", 1)
        x2T_lo = event("x2T_lo", 1)
        pick = event("pick", 8)
        down_ready = event("down_ready", 1)
        inter_lo = event("inter_lo", 4)
        y_ready = event("y_ready", IT)
        rstd_ready = event("rstd_ready", 1)
        rstd2_ready = event("rstd2_ready", 1)
        res_biased = event("res_biased", 1)
        x2_biased = event("x2_biased", 1)
        o_lo = event("o_lo", NG)

        w_loaded = [ctx.enter_context(nc.semaphore(f"w_loaded{i}")) for i in range(4)]
        small_loaded = ctx.enter_context(nc.semaphore("small_loaded"))
        lora_loaded = ctx.enter_context(nc.semaphore("lora_loaded"))
        w_hi = ctx.enter_context(nc.semaphore("w_hi"))
        w_lo = ctx.enter_context(nc.semaphore("w_lo"))
        pool_const = ctx.enter_context(nc.semaphore("pool_const"))
        dve_const = ctx.enter_context(nc.semaphore("dve_const"))
        act_const = ctx.enter_context(nc.semaphore("act_const"))

        def wait(eng, sem, b, k=0):
            n, unit = per_of(sem)
            value = b * (n * unit) + (k + 1) * unit
            if isinstance(b, int) and value <= 0:
                return
            eng.wait_ge(sem, value)

        def per_of(sem):
            for name, s in sems.items():
                if s is sem:
                    return per[name]
            raise KeyError

        def as_f32(ap):
            return ap.bitcast(F32)

        def in_order(text):
            return [(what, at[0], int(at[1:])) for what, at in (entry.split() for entry in text.split(","))]

        TENSOR_ORDER = in_order(
            "apply b2, xT n0, k b3, scores b5, gate c0, q n0, scores b6, apply b3, downT c0, up c0, "
            "up c1, apply b4, up c2, scores b7, up c3, k n0, apply b5, apply b6, v n0, k n1, scores n0, "
            "v n1, apply b7, q n1, v n2, scores n1, y c0, y c1, q n2, k n2, scores n2, apply n0, "
            "scores n3, wo b0, wo b1, v n3, q n3, apply n1, scores n4, x2T b0")
        SCALAR_ORDER = in_order(
            "o c2, exp b0, v b1, q b1, probs b0, den c7, v b2, exp b1, q b2, probs b1, o c3, k b2, "
            "exp b2, probs b2, den b0, exp b3, v b3, q b3, probs b3, den b1, x2T c0, exp b4, xT n0, k b3, "
            "ctx n0, probs b4, den b2, o b0, q n0, exp b5, downT c0, probs b5, up c0, den b3, exp b6, "
            "up c1, up c2, den b4, probs b6, k n0, up c3, exp b7, den b5, o b1, probs b7, v n0, k n1, "
            "den b6")
        VECTOR_ORDER = in_order(
            "q b2, probs b1, x_stats n0, clip b2, k b2, x_norm n0, probs b2, x2 c0, norm b0, x2 c1, "
            "x2_stats c0, clip b3, v b3, x2_norm c0, q b3, probs b3, norm b1, clip b4, xT n0, x2T c0, "
            "k b3, ctx n0, probs b4, choose c0, q n0, clip b5, norm b2, probs b5, up c0, norm b3, up c1, "
            "clip b6, up c2, norm b4, probs b6, up c3, k n0, clip b7, norm b5, v n0, probs b7, k n1, "
            "clip n0, v n1, norm b6, q n1, probs n0, v n2, norm b7, y c0, y c1, clip n1")
        GPSIMD_ORDER = in_order(
            "x_rstd n0, residual c0, x2_rstd c0, x2_bias c0, o b0, o b1, o b2, o b3")
        FREES = {"q": q_lo, "k": k_lo, "v": v_lo, "xT": xT_lo, "wo": x2_ready, "x2T": x2T_hi,
                 "gate": down_ready, "downT": downT_ready, "up": inter_lo, "y": y_ready}
        order = [u for u in TENSOR_ORDER if u[0] in FREES]
        bank_of = {(what, k): i % 2 for i, (what, _, k) in enumerate(order)}

        def bank(what, k):
            return g_ps[bank_of[what, k]][:, :]

        def as_two(ps):
            return ps.rearrange("p (a n) -> p a n", a=2)

        def who_runs(t):
            if not isinstance(t, int):
                return "bcn"
            return ("b" if 0 <= t < B else "") + ("c" if 0 <= t - 1 < B else "") + ("n" if 0 <= t + 1 < B else "")

        def seq(t, who):
            return {"b": t, "c": t - 1, "n": t + 1}[who]

        def parts(t, table):
            return [(what, seq(t, who), k) for what, who, k in table if who in who_runs(t)]

        def wait_bank(pe, t, what, k):
            at = [(w, i) for w, _, i in order].index((what, k))
            mine = [u for u in order[:at] if bank_of[u[0], u[2]] == bank_of[what, k]]
            every = [u for u in order if bank_of[u[0], u[2]] == bank_of[what, k]]
            for t_of, units in ((t, mine), (t - 1, every), (t - 2, every)):
                units = [u for u in units if u[1] in who_runs(t_of)]
                if units:
                    before, who, i = units[-1]
                    wait(pe, FREES[before], seq(t_of, who), i)
                    return

        flat = {name: buf.rearrange(pat) for name, buf, pat in (
            ("exp_s", exp_s[:, :, :, :], "p h j t -> p (h j t)"), ("o_raw", o_raw[:, :, :], "p a t -> p (a t)"),
            ("x2", x2[:, :, :], "p i d -> p (i d)"), ("x2n", x2n[:, :, :], "p i d -> p (i d)"))}
        EARLY = [(w, src, k) for w, src in ((wq, Wq), (wk, Wkv[:, 0:INNER]), (wv, Wkv[:, INNER:2 * INNER]))
                 for k in range(KC)]
        LATE = [(w, src, i) for w, src in ((wo, Wo), (wi, wiT), (wf, woT)) for i in range(4)]
        NE, NL, NB = len(EARLY), len(LATE), F // 512

        def early_piece(n):
            w, src, k = EARLY[n]
            buf = flat["exp_s" if n % 2 == 0 else "o_raw"]
            return n % 2, buf, src[128 * k:128 * k + 128, :], [part[:, k, :] for part in w]

        def late_piece(n):
            w, src, i = LATE[n]
            width = w[0].shape[2]
            chunks = w[0].shape[1]
            buf = flat["x2" if n % 2 == 0 else "x2n"]
            if width < 512:
                n_c = 512 // width
                return (2 + n % 2, buf.rearrange("p (c n) -> p c n", c=n_c),
                        src.rearrange("(c p) n -> p c n", p=128)[:, n_c * i:n_c * i + n_c, :],
                        [part[:, n_c * i:n_c * i + n_c, :] for part in w])
            c, h = divmod(i, 4 // chunks)
            return (2 + n % 2, buf, src[128 * c:128 * c + 128, 512 * h:512 * h + 512],
                    [part[:, c, 512 * h:512 * h + 512] for part in w])

        block = ctx.enter_context(nc.Block())

        @block.sync
        def _(sp):
            def load_x(b):
                wait(sp, xT_mm, b, -1)
                sp.dma_start(x_in[:, :, :], x[bass.ds(b, 1), :, :].rearrange("a (i p) d -> p (a i) d", p=128)) \
                    .then_inc(x_loaded, 16)

            def load_ctx(b):
                wait(sp, ctx_lo, b, -1)
                sp.dma_start(c_in[:, :, :], ctxT[bass.ds(b, 1), :, :, :].rearrange("a p k m -> p (a k) m")) \
                    .then_inc(ctx_loaded, 16)

            def load_residual(b):
                wait(sp, y_ready, b, -1)
                sp.dma_start(x2[:, :, :], x[bass.ds(b, 1), :, :].rearrange("a (i p) d -> p (a i) d", p=128)) \
                    .then_inc(res_loaded, 16)

            def store(b):
                wait(sp, y_ready, b, IT - 1)
                sp.dma_start(out[bass.ds(b, 1), :, :].rearrange("a (i p) d -> p (a i) d", p=128), x2n[:, :, :]) \
                    .then_inc(y_stored, 16)

            def iteration(t):
                who = who_runs(t)
                if "n" in who:
                    load_x(seq(t, "n"))
                    load_ctx(seq(t, "n"))
                if "c" in who:
                    store(seq(t, "c"))
                if "b" in who:
                    load_residual(seq(t, "b"))

            def load(piece):
                k, buf, src, _ = piece
                sp.dma_start(buf, src).then_inc(w_loaded[k], 16)

            load_x(0)
            for n in range(2):
                load(early_piece(n))
            load_ctx(0)
            sp.dma_start(gates[:, 0:1], g_xattn[0:1, :].to_broadcast([128, 1])).then_inc(small_loaded, 16)
            sp.dma_start(gates[:, 1:2], g_ffn[0:1, :].to_broadcast([128, 1])).then_inc(small_loaded, 16)
            sp.dma_start(mask_u8[:, :], mask).then_inc(small_loaded, 16)
            sp.dma_start(bo_row[:, :], bo[0:1, :].to_broadcast([128, D])).then_inc(small_loaded, 16)
            sp.dma_start(fb_row[:, :], wo_b[0:1, :].to_broadcast([128, D])).then_inc(small_loaded, 16)
            sp.dma_start(gb_row[:, :], gate_b[0:1, :].to_broadcast([128, E])).then_inc(small_loaded, 16)
            sp.dma_start(gate_w[:, :, :], gateA.rearrange("(k p) n -> p k n", p=128)).then_inc(small_loaded, 16)
            for n in range(2, NE):
                sp.wait_ge(w_lo, n - 1)
                load(early_piece(n))
            sp.wait_ge(pool_const, NB)
            for n in range(NB):
                buf, cols = flat["x2" if n % 2 == 0 else "x2n"], slice(512 * n, 512 * n + 512)
                for q in range(3):
                    sp.dma_start(buf[ER * q:ER * q + ER, :], loraB[:, cols]).then_inc(lora_loaded, 16)
                sp.dma_start(buf[96:98, :], wi_b[0:1, cols].to_broadcast([2, 512])).then_inc(lora_loaded, 16)
            load_x(1)
            load_ctx(1)
            for n in range(NL):
                sp.wait_ge(w_lo, NE + 1 + n)
                load(late_piece(n))
            sp.wait_ge(w_lo, NE + NB + NL)
            load_residual(0)
            iteration(1)
            with sp.Fori(2, B - 1) as t:
                iteration(t)
            iteration(B - 1)
            iteration(B)
            wait(sp, y_stored, B - 1)

        @block.gpsimd
        def _(pool):
            pool.memset(x2[96:128, :, :], 0.0).then_inc(pool_const, 1)
            pool.memset(x2n[96:128, :, :], 0.0).then_inc(pool_const, 1)
            pool.wait_ge(pool_const, 2)
            pool.memset(ident[:, :], 0.0).then_inc(pool_const, 1)
            pool.memset(lo_rows[:, :], 0.0).then_inc(pool_const, 1)
            pool.memset(neg_half[:, :], -0.5).then_inc(pool_const, 1)
            for e in range(E):
                last = pool.memset(rank[:, :, e:e + 1], float(E - e))
            last.then_inc(pool_const, 1)
            pool.wait_ge(pool_const, 6)
            pool.affine_select(out=ident[:, :], in_=ident[:, :], compare_op=ALU.not_equal, fill=1.0,
                               base=0, pattern=[[-1, 128]], channel_multiplier=1).then_inc(pool_const, 1)
            pool.wait_ge(pool_const, 7)
            pool.memset(lo_rows[2 * ER:3 * ER, :], -1.0).then_inc(pool_const, 1)
            pool.wait_ge(pool_const, 8)
            pool.affine_select(out=lo_rows[:, :], in_=lo_rows[:, :], compare_op=ALU.not_equal, fill=-1.0,
                               base=-97, pattern=[[0, 1]], channel_multiplier=1).then_inc(pool_const, 1)

            def rstd_of(out_, var, ready, done, b):
                wait(pool, ready, b)
                pool.tensor_tensor(out_[:, :], var[:, :], neg_half[:, :], ALU.pow).then_inc(done, 1)

            def split_o(b, g):
                wait(pool, wo_mm, b, -1)
                wait(pool, o_hi, b, g)
                s = 2 * (g % 2)
                pool.tensor_tensor(oT[1][:, 2 * g:2 * g + 2, :], o_raw[:, s:s + 2, :],
                                   as_f32(oT[0][:, 2 * g:2 * g + 2, :]), ALU.subtract).then_inc(o_lo, 1)

            def iteration(t):
                for what, s, k in parts(t, GPSIMD_ORDER):
                    if what == "o":
                        split_o(s, k)
                    elif what == "residual":
                        wait(pool, res_loaded, s)
                        pool.tensor_tensor(x2[:, :, :], x2[:, :, :], bo_row[:, None, :].to_broadcast([128, IT, D]),
                                           ALU.add).then_inc(res_biased, 1)
                    elif what == "x_rstd":
                        rstd_of(rstd, var_eps, var_ready, rstd_ready, s)
                    elif what == "x2_rstd":
                        rstd_of(rstd2, var_eps2, var2_ready, rstd2_ready, s)
                    elif what == "x2_bias":
                        wait(pool, x2_normed, s)
                        pool.tensor_tensor(x2[:, :, :], x2[:, :, :], fb_row[:, None, :].to_broadcast([128, IT, D]),
                                           ALU.add).then_inc(x2_biased, 1)

            pool.wait_ge(dve_const, 6)
            iteration(-1)
            iteration(0)
            iteration(1)
            with pool.Fori(2, B - 1) as t:
                iteration(t)
            iteration(B - 1)
            iteration(B)

        @block.scalar
        def _(act):
            def evac(out_, in_, done, func=ACT.Copy):
                act.activation(out_, in_, func).then_inc(done, 1)

            def exps(b, p):
                wait(act, s_mm, b, p)
                wait(act, probs_lo, b, p - 1)
                act.activation(exp_s[:, :, :, :], s_ps[p % 2][:, :, :, :], ACT.Exp, scale=SCALE) \
                    .then_inc(exp_done, 1)

            def copy_den(b, p):
                wait(act, pv_mm, b, p)
                wait(act, o_lo, b, p // 2 - 2)
                slot = p % 4
                act.activation(o_raw[0:64, slot, :], o_ps[p % 2][64:128, 0, :], ACT.Copy)
                act.activation(o_raw[64:128, slot, :], o_ps[p % 2][0:64, 1, :], ACT.Copy).then_inc(den_copied, 1)

            def split_o(b, g):
                wait(act, wo_mm, b, -1)
                wait(act, o_normed, b, 2 * g + 1)
                s = 2 * (g % 2)
                evac(oT[0][:, 2 * g:2 * g + 2, :], o_raw[:, s:s + 2, :], o_hi)

            def part(what, s, k):
                src = bank(what, k) if what in FREES else None
                if what == "exp":
                    exps(s, k)
                elif what == "probs":
                    wait(act, clipped, s, k)
                    wait(act, pv_mm, s, k - 2)
                    evac(probs[0][:, k % 2, :, :, :], exp_s[:, :, :, :], probs_hi)
                elif what == "den":
                    copy_den(s, k)
                elif what == "o":
                    split_o(s, k)
                elif what == "ctx":
                    split_ctx(s)
                elif what == "q":
                    wait(act, q_mm, s, k)
                    wait(act, s_mm, s, 2 * k - 3)
                    evac(qT[0][:, k % 2, :, :], src.rearrange("p (a t) -> p a t", a=2), q_hi)
                elif what == "k":
                    wait(act, k_mm, s, k)
                    wait(act, s_mm, s, 2 * k - 3)
                    evac(kT[0][:, k % 2, :, :], src.rearrange("p (a t) -> p a t", a=2), k_hi)
                elif what == "v":
                    half, j = divmod(k, 2)
                    wait(act, v_mm, s, k)
                    wait(act, pv_mm, s, NP // 2 * (half + 1) - 1 - NP)
                    evac(v[0][:, j, 4 * half:4 * half + 4, 0:3:2, :],
                         src.rearrange("p (a b d) -> p a b d", b=2, d=DH), v_hi)
                elif what == "xT":
                    wait(act, xT_mm, s)
                    wait(act, q_mm, s, -1)
                    evac(xT[0][:, :, :], src.rearrange("p (k t) -> p k t", k=KC), xT_hi)
                elif what == "x2T":
                    wait(act, x2T_mm, s)
                    act.activation(x2T_full, src.rearrange("p (k t) -> p k t", k=KC), ACT.Copy)
                    evac(x2T[0][:, :, :], src.rearrange("p (k t) -> p k t", k=KC), x2T_hi)
                elif what == "downT":
                    wait(act, downT_mm, s)
                    evac(downT[:, :], src[:, 0:T], downT_ready)
                elif what == "up":
                    wait(act, up_mm, s, k)
                    wait(act, y_mm, s, -1)
                    evac(inter[0][:, 2 * k:2 * k + 2, :], src.rearrange("p (f t) -> p f t", f=2), inter_hi, ACT.Relu)

            def split_ctx(b):
                wait(act, ctx_loaded, b)
                wait(act, k_mm, b, -1)
                wait(act, v_mm, b, -1)
                evac(cT[0][:, :, :], c_in[:, :, :], ctx_hi)

            def split_piece(piece, n_th):
                k, buf, _, (hi, _) = piece
                act.wait_ge(w_loaded[k], 16 * n_th)
                evac(hi, buf, w_hi)

            def iteration(t):
                at = 0
                for what, s, k in parts(t, SCALAR_ORDER):
                    part(what, s, k)
                    if isinstance(t, int) and t == 0 and what in ("probs", "den") and at < NL:
                        split_piece(late_piece(at), at // 2 + 1)
                        at += 1

            for n in range(NE):
                split_piece(early_piece(n), n // 2 + 1)
            act.wait_ge(small_loaded, 16 * 7)
            act.activation(tgate[:, :], gates[:, :], ACT.Tanh).then_inc(act_const, 1)
            act.wait_ge(lora_loaded, 16 * 4 * NB)
            for n in range(NB):
                evac(lora_w[:, 512 * n:512 * n + 512], flat["x2" if n % 2 == 0 else "x2n"], w_hi)
            iteration(-1)
            iteration(0)
            iteration(1)
            with act.Fori(2, B - 1) as t:
                iteration(t)
            iteration(B - 1)
            iteration(B)

        @block.tensor
        def _(pe):
            def three(out_, lhs, rhs, cut_l, cut_r, start, stop):
                pe.matmul(out_, cut_l(lhs[0]), cut_r(rhs[0]), start=start, stop=False)
                pe.matmul(out_, cut_l(lhs[0]), cut_r(rhs[1]), start=False, stop=False)
                return pe.matmul(out_, cut_l(lhs[1]), cut_r(rhs[0]), start=False, stop=stop)

            def scores(b, p):
                wait(pe, exp_done, b, p - 2)
                wait(pe, q_lo, b, p // 2)
                wait(pe, k_lo, b, p // 2)
                slot, a = p // 2 % 2, p % 2
                ps = s_ps[p % 2]
                for j in range(JC):
                    for part, (l, r) in enumerate(((0, 0), (0, 1), (1, 0))):
                        for h in range(2):
                            rows = slice(64 * h, 64 * h + 64)
                            last = pe.matmul(ps[:, h, j, :], kT[l][rows, slot, a, 128 * j:128 * j + 128],
                                             qT[r][rows, slot, a, :], start=(part == 0), stop=(part == 2))
                last.then_inc(s_mm, 1)

            def apply(b, p):
                wait(pe, probs_lo, b, p)
                wait(pe, o_normed, b, p - 2)
                wait(pe, v_lo, b, 1 + 2 * (p // (NP // 2)))
                for h in range(2):
                    for j in range(JC):
                        last = three(o_ps[p % 2][:, h, :], v, probs,
                                     lambda w: w[:, j, p, h:h + 2, :].rearrange("k a d -> k (a d)"),
                                     lambda w: w[:, p % 2, h, j, :], j == 0, j == JC - 1)
                last.then_inc(pv_mm, 1)

            def unit(t, what, s, k):
                ps = bank(what, k)
                wait_bank(pe, t, what, k)
                if what == "q":
                    wait(pe, xT_lo, s)
                    if isinstance(s, int) and s == 0:
                        pe.wait_ge(w_lo, KC)
                    for a in range(2):
                        cols = slice(128 * (2 * k + a), 128 * (2 * k + a) + 128)
                        for c in range(KC):
                            last = three(ps[:, T * a:T * a + T], wq, xT, lambda w: w[:, c, cols],
                                         lambda w: w[:, c, :], c == 0, c == KC - 1)
                    last.then_inc(q_mm, 1)
                elif what == "k":
                    wait(pe, ctx_lo, s)
                    if isinstance(s, int) and s == 0:
                        pe.wait_ge(w_lo, 2 * KC)
                    for a in range(2):
                        cols = slice(128 * (2 * k + a), 128 * (2 * k + a) + 128)
                        for c in range(KC):
                            last = three(ps[:, M * a:M * a + M], wk, cT, lambda w: w[:, c, cols],
                                         lambda w: w[:, c, :], c == 0, c == KC - 1)
                    last.then_inc(k_mm, 1)
                elif what == "v":
                    half, j = divmod(k, 2)
                    wait(pe, ctx_lo, s)
                    if isinstance(s, int) and s == 0:
                        pe.wait_ge(w_lo, 3 * KC)
                    for c in range(KC):
                        last = three(ps[:, :], cT, wv, lambda w: w[:, c, 128 * j:128 * j + 128],
                                     lambda w: w[:, c, 512 * half:512 * half + 512], c == 0, c == KC - 1)
                    last.then_inc(v_mm, 1)
                elif what == "xT":
                    wait(pe, x_normed, s)
                    for c in range(KC):
                        for i in range(IT):
                            last = pe.transpose(ps[:, T * c + 128 * i:T * c + 128 * i + 128],
                                                x_in[:, i, 128 * c:128 * c + 128], ident[:, :])
                    last.then_inc(xT_mm, 1)
                elif what == "wo":
                    wait(pe, o_lo, s, NG - 1)
                    if isinstance(s, int) and s == 0:
                        pe.wait_ge(w_lo, NE + NB + NL // 3)
                    for c in range(NP):
                        last = three(ps[:, 0:D], oT, wo, lambda w: w[:, c, 128 * k:128 * k + 128],
                                     lambda w: w[:, c, :], c == 0, c == NP - 1)
                    last.then_inc(wo_mm, 1)
                elif what == "x2T":
                    wait(pe, x2_normed, s)
                    for c in range(KC):
                        for i in range(IT):
                            last = pe.transpose(ps[:, T * c + 128 * i:T * c + 128 * i + 128],
                                                x2n[:, i, 128 * c:128 * c + 128], ident[:, :])
                    last.then_inc(x2T_mm, 1)
                elif what == "gate":
                    wait(pe, x2T_hi, s)
                    for i in range(IT):
                        for c in range(KC):
                            last = pe.matmul(ps[:, 64 * i:64 * i + GA], x2T_full[:, c, 128 * i:128 * i + 128],
                                             gate_w[:, c, :], start=(c == 0), stop=(c == KC - 1))
                    last.then_inc(gate_mm, 1)
                elif what == "downT":
                    wait(pe, down_ready, s)
                    for i in range(IT):
                        last = pe.transpose(ps[:, 128 * i:128 * i + 128], as_f32(down_s[:, i, :]), ident[:, :])
                    last.then_inc(downT_mm, 1)
                elif what == "up":
                    wait(pe, x2T_lo, s)
                    if isinstance(s, int) and s == 0:
                        pe.wait_ge(w_lo, NE + NB + 2 * NL // 3)
                    for a in range(2):
                        cols = slice(128 * (2 * k + a), 128 * (2 * k + a) + 128)
                        o = ps[:, T * a:T * a + T]
                        for c in range(KC):
                            three(o, wi, x2T, lambda w: w[:, c, cols], lambda w: w[:, c, :], c == 0, False)
                        wait(pe, downT_ready, s)
                        last = pe.matmul(o, lora_w[:, cols], downT[:, :], start=False, stop=True)
                    last.then_inc(up_mm, 1)
                elif what == "y":
                    wait(pe, inter_lo, s, 3)
                    if isinstance(s, int) and s == 0:
                        pe.wait_ge(w_lo, NE + NB + NL)
                    for f in range(FC):
                        last = three(ps[:, 0:D], inter, wf, lambda w: w[:, f, 128 * k:128 * k + 128],
                                     lambda w: w[:, f, :], f == 0, f == FC - 1)
                    last.then_inc(y_mm, 1)

            def iteration(t):
                for what, s, k in parts(t, TENSOR_ORDER):
                    if what == "scores":
                        scores(s, k)
                    elif what == "apply":
                        apply(s, k)
                    else:
                        unit(t, what, s, k)

            pe.wait_ge(pool_const, 7)
            iteration(-1)
            pe.wait_ge(dve_const, 6)
            iteration(0)
            iteration(1)
            with pe.Fori(2, B - 1) as t:
                iteration(t)
            iteration(B - 1)
            iteration(B)

        @block.vector
        def _(dve):
            def sub(out_, in_, hi, done):
                dve.tensor_tensor(out_, in_, as_f32(hi), ALU.subtract).then_inc(done, 1)

            def clip(b, p):
                wait(dve, exp_done, b, p)
                wait(dve, bound_set, b)
                for j in range(JC):
                    e = exp_s[:, :, j, :]
                    last = dve.tensor_scalar(e, e, bound_b[:, 0, j:j + 1], LO_BOUND, ALU.min, ALU.max)
                last.then_inc(clipped, 1)

            def norm_o(b, p):
                slot = p % 4
                wait(dve, den_copied, b, p)
                dve.transpose(den_T[:, :], o_raw[:, slot, :]).then_inc(den_turned, 1)
                wait(dve, den_turned, b, p)
                dve.reciprocal(den_inv[:, :], den_T[:, 0:T:32]).then_inc(inverted, 1)
                wait(dve, inverted, b, p)
                dve.transpose(o_raw[:, slot, :].rearrange("p (a b) -> p a b", b=32),
                              den_inv[:, :, None].to_broadcast([128, T // 32, 32])).then_inc(inv_spread, 1)
                wait(dve, inv_spread, b, p)
                dve.tensor_tensor(o_raw[0:64, slot, :], o_ps[p % 2][0:64, 0, :], o_raw[0:64, slot, :], ALU.mult)
                dve.tensor_tensor(o_raw[64:128, slot, :], o_ps[p % 2][64:128, 1, :], o_raw[64:128, slot, :],
                                  ALU.mult).then_inc(o_normed, 1)

            def layer_stats(src, st, mo, ve, done, mdone, ready, b):
                for i in range(IT):
                    dve.bn_stats(st[:, i, :], src[:, i, :]).then_inc(done, 1)
                wait(dve, done, b, IT - 1)
                dve.tensor_copy(ve[:, 0:1], st[:, IT - 1, 0:1])
                for i in range(IT):
                    dve.bn_aggr(mo[:, i, :], st[:, i, :]).then_inc(mdone, 1)
                wait(dve, mdone, b, IT - 1)
                dve.tensor_scalar(ve[:, :], mo[:, :, 1], EPS, None, ALU.add).then_inc(ready, 1)

            def normalise(dst, src, mo, rs, ready, done, b):
                wait(dve, ready, b)
                for i in range(IT):
                    last = dve.tensor_scalar(dst[:, i, :], src[:, i, :], mo[:, i, 0:1], rs[:, i:i + 1],
                                             ALU.subtract, ALU.mult)
                last.then_inc(done, 1)

            FROM = {"choose": "gate", "x2": "wo"}

            def choose(b, ps):
                g = ps[:, 0:128].rearrange("p (i n) -> p i n", i=IT)
                wait(dve, gate_mm, b)
                dve.tensor_tensor(logits[:, :, :], g[:, :, 0:E], gb_row[:, None, :].to_broadcast([128, IT, E]),
                                  ALU.add).then_inc(pick, 1)
                wait(dve, pick, b, 0)
                dve.tensor_reduce(top[:, :], logits[:, :, :], AX.X, ALU.max).then_inc(pick, 1)
                wait(dve, pick, b, 1)
                dve.tensor_tensor(ranked[:, :, :], logits[:, :, :], top[:, :, None].to_broadcast([128, IT, E]),
                                  ALU.is_equal).then_inc(pick, 1)
                wait(dve, pick, b, 2)
                dve.tensor_tensor(ranked[:, :, :], ranked[:, :, :], rank[:, :, :], ALU.mult).then_inc(pick, 1)
                wait(dve, pick, b, 3)
                dve.tensor_reduce(first[:, :], ranked[:, :, :], AX.X, ALU.max).then_inc(pick, 1)
                wait(dve, pick, b, 4)
                dve.tensor_tensor(chosen[:, :, :], ranked[:, :, :], first[:, :, None].to_broadcast([128, IT, E]),
                                  ALU.is_equal).then_inc(pick, 1)
                wait(dve, pick, b, 5)
                for i in range(IT):
                    last = dve.tensor_tensor(down[:, i, :].rearrange("p (e r) -> p e r", r=R),
                                             g[:, i, E:GA].rearrange("p (e r) -> p e r", r=R),
                                             chosen[:, i, :, None].to_broadcast([128, E, R]), ALU.mult)
                last.then_inc(pick, 1)
                wait(dve, pick, b, 6)
                wait(dve, downT_mm, b, -1)
                dve.tensor_copy(down_s[:, :, 2 * ER:3 * ER], down[:, :, :])
                dve.tensor_copy(down_s[:, :, 0:ER], down[:, :, :]).then_inc(pick, 1)
                wait(dve, pick, b, 7)
                sub(down_s[:, :, ER:2 * ER], down[:, :, :], down_s[:, :, 0:ER], down_ready)

            def part(what, s, k):
                src = bank(FROM.get(what, what), k) if FROM.get(what, what) in FREES else None
                two = as_two(src) if src is not None else None
                if what == "clip":
                    if k == 0:
                        wait(dve, clipped, s, -1)
                        dve.tensor_copy(bound_b[:, 0, :], bound[:, bass.ds(s * JC, JC)]).then_inc(bound_set, 1)
                    clip(s, k)
                elif what == "probs":
                    wait(dve, probs_hi, s, k)
                    sub(probs[1][:, k % 2, :, :, :], exp_s[:, :, :, :], probs[0][:, k % 2, :, :, :], probs_lo)
                elif what == "norm":
                    norm_o(s, k)
                elif what == "x_stats":
                    wait(dve, x_loaded, s)
                    layer_stats(x_in, stats, moments, var_eps, stats_done, moments_done, var_ready, s)
                elif what == "x2_stats":
                    wait(dve, x2_ready, s, IT - 1)
                    layer_stats(x2, stats2, moments2, var_eps2, stats2_done, moments2_done, var2_ready, s)
                elif what == "x_norm":
                    normalise(x_in, x_in, moments, rstd, rstd_ready, x_normed, s)
                elif what == "x2_norm":
                    wait(dve, y_stored, s, -1)
                    normalise(x2n, x2, moments2, rstd2, rstd2_ready, x2_normed, s)
                elif what == "ctx":
                    split_ctx(s)
                elif what == "v":
                    half, j = divmod(k, 2)
                    wait(dve, v_hi, s, k)
                    cols = slice(4 * half, 4 * half + 4)
                    sub(v[1][:, j, cols, 0:3:2, :], src.rearrange("p (a b d) -> p a b d", b=2, d=DH),
                        v[0][:, j, cols, 0:3:2, :], v_lo)
                elif what == "q":
                    wait(dve, q_hi, s, k)
                    sub(qT[1][:, k % 2, :, :], two, qT[0][:, k % 2, :, :], q_lo)
                elif what == "k":
                    wait(dve, k_hi, s, k)
                    sub(kT[1][:, k % 2, :, :], two, kT[0][:, k % 2, :, :], k_lo)
                elif what == "xT":
                    wait(dve, xT_hi, s)
                    sub(xT[1][:, :, :], two, xT[0][:, :, :], xT_lo)
                elif what == "x2":
                    wait(dve, wo_mm, s, k)
                    wait(dve, res_biased, s)
                    dve.scalar_tensor_tensor(x2[:, k, :], src[:, 0:D], tgate[:, 0:1], x2[:, k, :],
                                             ALU.mult, ALU.add).then_inc(x2_ready, 1)
                elif what == "x2T":
                    wait(dve, x2T_hi, s)
                    sub(x2T[1][:, :, :], x2T_full, x2T[0][:, :, :], x2T_lo)
                elif what == "choose":
                    choose(s, src)
                elif what == "up":
                    wait(dve, inter_hi, s, k)
                    dve.scalar_tensor_tensor(inter[1][:, 2 * k:2 * k + 2, :], two, 0.0,
                                             as_f32(inter[0][:, 2 * k:2 * k + 2, :]), ALU.max,
                                             ALU.subtract).then_inc(inter_lo, 1)
                elif what == "y":
                    wait(dve, y_mm, s, k)
                    wait(dve, x2_biased, s)
                    dve.scalar_tensor_tensor(x2n[:, k, :], src[:, 0:D], tgate[:, 1:2], x2[:, k, :],
                                             ALU.mult, ALU.add).then_inc(y_ready, 1)

            def split_ctx(b):
                wait(dve, ctx_hi, b)
                sub(cT[1][:, :, :], c_in[:, :, :], cT[0][:, :, :], ctx_lo)

            def split_piece(piece, n):
                _, buf, _, (hi, lo) = piece
                dve.wait_ge(w_hi, n)
                sub(lo, buf, hi, w_lo)

            def iteration(t):
                at = 0
                for what, s, k in parts(t, VECTOR_ORDER):
                    part(what, s, k)
                    if isinstance(t, int) and t == 0 and what in ("probs", "norm") and at < NL:
                        split_piece(late_piece(at), NE + NB + at + 1)
                        at += 1

            dve.wait_ge(small_loaded, 16 * 7)
            dve.tensor_scalar(bound[:, :], mask_u8[:, :], HI_BOUND - LO_BOUND, LO_BOUND, ALU.mult, ALU.add) \
                .then_inc(dve_const, 1)
            dve.memset(as_f32(down_s[:, :, 96:98]), 1.0)
            dve.memset(as_f32(down_s[:, :, 98:128]), 0.0).then_inc(dve_const, 1)
            dve.memset(as_f32(v[0][:, :, :, 1, :]), 1.0).then_inc(dve_const, 1)
            dve.memset(as_f32(v[1][:, :, :, 1, :]), 0.0).then_inc(dve_const, 1)
            for n in range(NE):
                split_piece(early_piece(n), n + 1)
            dve.wait_ge(act_const, 1)
            dve.tensor_scalar(bo_row[:, :], bo_row[:, :], tgate[:, 0:1], None, ALU.mult).then_inc(dve_const, 1)
            dve.tensor_scalar(fb_row[:, :], fb_row[:, :], tgate[:, 1:2], None, ALU.mult).then_inc(dve_const, 1)
            dve.wait_ge(pool_const, 9)
            for n in range(NB):
                dve.wait_ge(w_hi, NE + n + 1)
                cols = slice(512 * n, 512 * n + 512)
                dve.scalar_tensor_tensor(lora_w[:, cols], as_f32(lora_w[:, cols]), lo_rows[:, 0:1],
                                         flat["x2" if n % 2 == 0 else "x2n"], ALU.mult, ALU.add).then_inc(w_lo, 1)
            iteration(-1)
            iteration(0)
            iteration(1)
            with dve.Fori(2, B - 1) as t:
                iteration(t)
            iteration(B - 1)
            iteration(B)


def kernel(**inputs):
    import numpy as _np
    import concourse.bacc as _bacc
    from concourse import mybir as _mybir
    from concourse.bass_utils import run_bass_kernel_spmd as _run

    a = {k: _np.asarray(v) for k, v in inputs.items()}
    B, M, D = a["ctx_1024"].shape
    E, R, _ = a["L0_ffn_lora_A"].shape
    F = a["L0_ffn_wi_W"].shape[0]
    feeds = {
        "x": a["x"],
        "ctxT": a["ctx_1024"].reshape(B, M, D // 128, 128).transpose(0, 3, 2, 1),
        "mask": a["mask_BxS2_bk1"].reshape(B, M // 128, 128).transpose(2, 0, 1).reshape(128, -1),
        "g_xattn": a["g_xattn"].reshape(1, 1),
        "g_ffn": a["g_ffn"].reshape(1, 1),
        "Wq": a["L0_xattn_Wq"],
        "Wkv": a["L0_xattn_Wkv"],
        "Wo": a["L0_xattn_Wo"],
        "bo": a["L0_xattn_bo"].reshape(1, -1),
        "gateA": _np.concatenate([a["L0_ffn_gate_W"].T, a["L0_ffn_lora_A"].reshape(E * R, D).T], axis=1),
        "gate_b": a["L0_ffn_gate_b"].reshape(1, -1),
        "wiT": a["L0_ffn_wi_W"].T,
        "wi_b": a["L0_ffn_wi_b"].reshape(1, -1),
        "woT": a["L0_ffn_wo_W"].T,
        "wo_b": a["L0_ffn_wo_b"].reshape(1, -1),
        "loraB": a["L0_ffn_lora_B"].transpose(0, 2, 1).reshape(E * R, F),
    }
    nc = _bacc.Bacc("TRN2", target_bir_lowering=False, num_devices=1, dynamic_dma_scratch_size=512)
    arrays, args = {}, []
    for name, value in feeds.items():
        value = _np.ascontiguousarray(value)
        arrays[f"in_{name}"] = value
        args.append(nc.dram_tensor(f"in_{name}", value.shape, _mybir.dt.from_np(value.dtype),
                                   kind="ExternalInput").ap())
    out = nc.dram_tensor("out_y", a["x"].shape, _mybir.dt.float32, kind="ExternalOutput").ap()
    gated_cross_attention_and_lora_ffn(nc, *args, out)
    r = _run(nc, [arrays], core_ids=[0])
    return r.results[0]["out_y"]
```

```python
import concourse.bass as bass
from concourse import mybir
from contextlib import ExitStack


def gated_cross_attention_and_lora_ffn(nc, x, ctxT, mask, g_xattn, g_ffn, Wq, Wkv, Wo, bo, gateA, gate_b,
                                       wiT, wi_b, woT, wo_b, loraB, out):
    F32, F32R, U8 = mybir.dt.float32, mybir.dt.float32r, mybir.dt.uint8
    ALU, ACT, AX = mybir.AluOpType, mybir.ActivationFunctionType, mybir.AxisListType

    B, T, D = x.shape
    M = ctxT.shape[3]
    INNER = Wq.shape[1]
    DH = 64
    H = INNER // DH
    NP = H // 2
    NG = NP // 2
    KC = D // 128
    JC = M // 128
    IT = T // 128
    F = wiT.shape[1]
    FC = F // 128
    E, ER = gate_b.shape[1], loraB.shape[0]
    R = ER // E
    GA = E + ER
    SCALE = DH ** -0.5
    LO_BOUND, HI_BOUND = 0.006737947, 148.41316
    EPS = 1e-5

    with ExitStack() as ctx:
        def sb(name, shape, dt=F32):
            return ctx.enter_context(nc.sbuf_tensor(name, shape, dt))

        def pair_of(name, shape):
            return sb(name + "_hi", shape, F32R), sb(name + "_lo", shape, F32R)

        with ExitStack() as loading:
            w_buf = [loading.enter_context(nc.sbuf_tensor(f"w_buf{i}", [128, D * INNER // 256], F32))
                     for i in range(8)]
        inter = pair_of("inter", [128, FC, T])
        oT = pair_of("oT", [128, NP, T])

        wq = pair_of("wq", [128, KC, INNER])
        wk = pair_of("wk", [128, KC, INNER])
        wv = pair_of("wv", [128, KC, INNER])
        wo = pair_of("wo", [128, NP, D])
        wi = pair_of("wi", [128, KC, F])
        wf = pair_of("wf", [128, FC, D])
        lora_w = sb("lora_w", [128, F], F32R)
        gate_w = pair_of("gate_w", [128, KC, GA])

        ident = sb("ident", [128, 128])
        neg_half = sb("neg_half", [128, IT])
        rank = sb("rank", [128, IT, E])
        lo_rows = sb("lo_rows", [128, 1])
        gates = sb("gates", [128, 2])
        tgate = sb("tgate", [128, 2])
        bo_row = sb("bo_row", [128, D])
        fb_row = sb("fb_row", [128, D])
        gb_row = sb("gb_row", [128, E])
        mask_u8 = sb("mask_u8", [128, B * JC], U8)
        bound = sb("bound", [128, B * JC])
        bound_b = sb("bound_b", [128, JC])

        x_in = sb("x_in", [128, IT, D])
        stats = sb("stats", [128, IT, 6])
        moments = sb("moments", [128, IT, 2])
        var_eps = sb("var_eps", [128, IT])
        rstd = sb("rstd", [128, IT])
        xT = pair_of("xT", [128, KC, T])
        c_in = sb("c_in", [128, KC, M])
        cT = pair_of("cT", [128, KC, M])
        q_parts = sb("q_parts", [128, 2, 2, 2, T], F32R)
        k_twice = sb("k_twice", [128, 2, 2, 2, M], F32R)
        kT_lo = sb("kT_lo", [128, 2, 2, M], F32R)
        HEAD_ROWS = [slice(0, 64), slice(64, 128)]
        v = pair_of("v", [128, JC, NP, 3, DH])
        with ExitStack() as before_split:
            exp_s = before_split.enter_context(nc.sbuf_tensor("exp_s", [128, 2, 2, JC, T], F32))
        probs_lo_part = sb("probs_lo_part", [128, 2, 2, JC, T], F32R)
        probs = sb("probs_hi_part", [128, 2, 2, JC, T], F32R), probs_lo_part
        den_T = sb("den_T", [128, T])
        den_inv = sb("den_inv", [128, T // 32])
        o_raw = sb("o_raw", [128, 4, T])

        x2 = sb("x2", [128, IT, D])
        stats2 = sb("stats2", [128, IT, 6])
        moments2 = sb("moments2", [128, IT, 2])
        var_eps2 = sb("var_eps2", [128, IT])
        rstd2 = sb("rstd2", [128, IT])
        x2n = sb("x2n", [128, IT, D])
        gateT = x2n[0:GA, 0, 0:T]
        down = x2n[:, 1, 0:IT * ER].rearrange("p (i n) -> p i n", i=IT)
        x2T = pair_of("x2T", [128, KC, T])
        logits = sb("logits", [128, IT, E])
        top = sb("top", [128, IT])
        ranked = sb("ranked", [128, IT, E])
        first = sb("first", [128, IT])
        chosen = sb("chosen", [128, IT, E])
        down_s = sb("down_s", [128, IT, 128], F32R)
        downT = sb("downT", [128, T], F32R)

        s_ps = [ctx.enter_context(nc.psum_tensor(f"s_ps{i}", [128, 2, JC, T], F32)) for i in range(2)]
        o_ps = [ctx.enter_context(nc.psum_tensor(f"o_ps{i}", [128, 2, T], F32)) for i in range(2)]
        g_ps = [ctx.enter_context(nc.psum_tensor(f"g_ps{i}", [128, 512], F32)) for i in range(2)]

        per, sems = {}, {}

        def event(name, n, dma=False):
            sems[name] = ctx.enter_context(nc.semaphore(name))
            per[name] = (n, 16 if dma else 1)
            return sems[name]

        x_loaded = event("x_loaded", 1, True)
        ctx_loaded = event("ctx_loaded", 1, True)
        res_loaded = event("res_loaded", 1, True)
        y_stored = event("y_stored", 1, True)
        q_mm = event("q_mm", NG)
        k_mm = event("k_mm", NG)
        v_mm = event("v_mm", 4)
        xT_mm = event("xT_mm", 1)
        s_mm = event("s_mm", NP)
        pv_mm = event("pv_mm", NP)
        wo_mm = event("wo_mm", IT)
        x2T_mm = event("x2T_mm", 1)
        gateT_mm = event("gateT_mm", 1)
        gate_mm = event("gate_mm", 1)
        downT_mm = event("downT_mm", 1)
        up_mm = event("up_mm", 4)
        y_mm = event("y_mm", IT)
        q_hi = event("q_hi", NG)
        k_hi = event("k_hi", NG)
        k_doubled = event("k_doubled", NG)
        v_hi = event("v_hi", 4)
        xT_hi = event("xT_hi", 1)
        ctx_hi = event("ctx_hi", 1)
        exp_done = event("exp_done", NP)
        probs_hi = event("probs_hi", NP)
        den_copied = event("den_copied", NP)
        o_hi = event("o_hi", NG)
        x2T_hi = event("x2T_hi", 1)
        gateT_ready = event("gateT_ready", 1)
        downT_ready = event("downT_ready", 1)
        inter_hi = event("inter_hi", 4)
        q_lo = event("q_lo", NG)
        k_lo = event("k_lo", NG)
        bound_set = event("bound_set", 1)
        stats_done = event("stats_done", 2)
        moments_done = event("moments_done", 2)
        var_ready = event("var_ready", 1)
        x_normed = event("x_normed", 1)
        xT_lo = event("xT_lo", 1)
        v_lo = event("v_lo", 4)
        clipped = event("clipped", NP)
        probs_lo = event("probs_lo", NP)
        den_turned = event("den_turned", NP)
        inverted = event("inverted", NP)
        inv_spread = event("inv_spread", NP)
        o_normed = event("o_normed", NP)
        x2_ready = event("x2_ready", IT)
        stats2_done = event("stats2_done", 2)
        moments2_done = event("moments2_done", 2)
        var2_ready = event("var2_ready", 1)
        x2_normed = event("x2_normed", 1)
        x2T_lo = event("x2T_lo", 1)
        pick = event("pick", 8)
        down_ready = event("down_ready", 1)
        inter_lo = event("inter_lo", 4)
        y_ready = event("y_ready", IT)
        ctx_lo = event("ctx_lo", 1)
        probs2_lo = event("probs2_lo", NP)
        rstd_ready = event("rstd_ready", 1)
        rstd2_ready = event("rstd2_ready", 1)
        res_biased = event("res_biased", 1)
        x2_biased = event("x2_biased", 1)
        o_lo = event("o_lo", NG)

        w_loaded = [ctx.enter_context(nc.semaphore(f"w_loaded{i}")) for i in range(15)]
        small_loaded = ctx.enter_context(nc.semaphore("small_loaded"))
        w_hi = ctx.enter_context(nc.semaphore("w_hi"))
        w_lo = ctx.enter_context(nc.semaphore("w_lo"))
        ident_zero = ctx.enter_context(nc.semaphore("ident_zero"))
        ident_ready = ctx.enter_context(nc.semaphore("ident_ready"))
        pool_const = ctx.enter_context(nc.semaphore("pool_const"))
        ones_set = ctx.enter_context(nc.semaphore("ones_set"))
        bounds_set = ctx.enter_context(nc.semaphore("bounds_set"))
        tanh_done = ctx.enter_context(nc.semaphore("tanh_done"))
        biases_scaled = ctx.enter_context(nc.semaphore("biases_scaled"))

        def wait(eng, sem, b, k=0):
            n, unit = per_of(sem)
            value = b * (n * unit) + (k + 1) * unit
            if isinstance(b, int) and value <= 0:
                return
            eng.wait_ge(sem, value)

        def per_of(sem):
            for name, s in sems.items():
                if s is sem:
                    return per[name]
            raise KeyError

        def as_f32(ap):
            return ap.bitcast(F32)

        def in_order(text):
            return [(what, at[0], int(at[1:])) for what, at in (entry.split() for entry in text.split(","))]

        TENSOR_START = in_order(
            "xT b0, q b0, k b0, q b1, scores b0, k b1, v b0, scores b1, v b1, q b2, scores b2, scores b3, "
            "apply b0, v b2, v b3, apply b1, k b2, q b3, apply b2, scores b4, xT n0, k b3, scores b5, q n0, "
            "apply b3, k n0, scores b6, scores b7, apply b4, q n1, apply b5, v n0, k n1, apply b6, scores n0")
        TENSOR_ORDER = in_order(
            "apply c7, scores b1, v b1, q b2, scores b2, v b2, apply b0, wo c0, wo c1, v b3, k b2, scores b3, "
            "q b3, apply b1, x2T c0, apply b2, gateT c0, xT n0, k b3, scores b4, scores b5, q n0, gate c0, "
            "apply b3, scores b6, scores b7, downT c0, up c0, up c1, up c2, up c3, k n0, apply b4, q n1, "
            "apply b5, k n1, y c0, apply b6, scores n0, y c1, v n0")
        TENSOR_END = in_order(
            "apply c7, scores b1, v b1, q b2, scores b2, v b2, apply b0, wo c0, wo c1, v b3, k b2, apply b1, "
            "scores b3, q b3, x2T c0, apply b2, scores b4, k b3, apply b3, scores b5, gateT c0, scores b6, "
            "gate c0, apply b4, scores b7, downT c0, up c0, up c1, apply b5, up c2, up c3, apply b6, apply b7, "
            "y c0, y c1, wo b0, wo b1, x2T b0, gateT b0, gate b0, downT b0, up b0, up b1, up b2, up b3, y b0, "
            "y b1")
        SCALAR_START = in_order(
            "w b0, w b1, xT b0, w b2, ctx b0, w b3, q b0, w b4, w b5, k b0, q b1, k_twice b0, w b6, w b7, w b8, "
            "exp b0, k b1, v b0, k_twice b1, exp b1, probs b0, v b1, q b2, w b9, probs b1, w b10, exp b2, v b2, "
            "w b11, den b0, probs b2, v b3, w b12, exp b3, k b2, den b1, k_twice b2, q b3, tanh b0, den b2, "
            "exp b4, xT n0, probs b3, k b3, ctx n0, probs b4, k_twice b3, den b3, q n0, exp b5, w b13, probs b5, "
            "exp b6, o b0, k n0, q n1, o b1, den b4, k_twice n0, probs b6, exp b7, den b5, v n0, probs b7, w b14, "
            "k n1, den b6, exp n0, k_twice n1, o b2, v n1, den b7, exp n1, probs n0, q n2, o b3, probs n1")
        SCALAR_ORDER = in_order(
            "v b2, den b0, exp b2, probs b2, v b3, k b2, k_twice b2, q b3, x2T c0, den b1, exp b3, gateT c0, "
            "xT n0, probs b3, k b3, exp b4, k_twice b3, ctx n0, q n0, exp b5, den b2, downT c0, den b3, up c0, "
            "probs b4, up c1, o b0, up c2, probs b5, up c3, k n0, exp b6, q n1, den b4, probs b6, k_twice n0, "
            "k n1, exp b7, o b1, den b5, probs b7, den b6, o b2, exp n0, v n0, k_twice n1, den b7, probs n0, "
            "v n1, exp n1, o b3, q n2, probs n1")
        SCALAR_END = in_order(
            "v b2, exp b2, den b0, probs b2, v b3, k b2, den b1, k_twice b2, exp b3, q b3, x2T c0, den b2, "
            "probs b3, exp b4, k b3, k_twice b3, probs b4, den b3, gateT c0, exp b5, exp b6, o b0, downT c0, "
            "probs b5, den b4, o b1, up c0, up c1, probs b6, exp b7, den b5, probs b7, up c2, up c3, den b6, "
            "o b2, den b7, o b3, x2T b0, gateT b0, downT b0, up b0, up b1, up b2, up b3")
        VECTOR_START = in_order(
            "x_stats b0, x_norm b0, w b0, w b1, xT b0, w b2, w b3, q b0, w b4, w b5, k b0, q b1, x_stats n0, "
            "w b6, bounds b0, clip b0, x_norm n0, v b0, k b1, w b7, probs b0, w b8, clip b1, v b1, q b2, w b9, "
            "probs b1, w b10, clip b2, v b2, norm b0, v b3, probs b2, w b11, k b2, norm b1, q b3, clip b3, "
            "clip b4, xT n0, probs b3, w b12, k b3, norm b2, probs b4, q n0, clip b5, norm b3, probs b5, w b13, "
            "biases b0, k n0, clip b6, q n1, norm b4, clip b7, probs b6, norm b5, probs b7, w b14, v n0, norm b6, "
            "clip n0, k n1, v n1, norm b7")
        VECTOR_ORDER = in_order(
            "probs b0, clip b1, q b2, x_stats n0, v b2, probs b1, clip b2, x2 c0, norm b0, x2 c1, x2_stats c0, "
            "v b3, probs b2, x2_norm c0, k b2, q b3, x2T c0, x_norm n0, clip b3, norm b1, xT n0, k b3, probs b3, "
            "choose c0, q n0, clip b4, norm b2, up c0, clip b5, up c1, probs b4, up c2, norm b3, up c3, probs b5, "
            "k n0, clip b6, q n1, norm b4, probs b6, k n1, clip b7, y c0, norm b5, probs b7, norm b6, v n0, "
            "clip n0, y c1, norm b7, v n1")
        VECTOR_END = in_order(
            "clip b1, probs b0, q b2, v b2, probs b1, clip b2, norm b0, x2 c0, probs b2, x2 c1, x2_stats c0, "
            "v b3, x2_norm c0, k b2, norm b1, clip b3, q b3, norm b2, probs b3, clip b4, x2T c0, k b3, probs b4, "
            "norm b3, choose c0, clip b5, clip b6, probs b5, norm b4, up c0, up c1, probs b6, clip b7, norm b5, "
            "probs b7, up c2, up c3, norm b6, norm b7, y c0, y c1, x2 b0, x2 b1, x2_stats b0, x2_norm b0, x2T b0, "
            "choose b0, up b0, up b1, up b2, up b3, y b0, y b1")
        GPSIMD_START = in_order(
            "x_rstd b0, ones b0, ctx b0, x_rstd n0, probs b0, probs b1, probs b2, probs b3, ctx n0, probs b4, "
            "o b0, probs b5, o b1, probs b6, probs b7, o b2, probs n0, o b3, residual b0, probs n1")
        GPSIMD_ORDER = in_order(
            "x2_rstd c0, probs b2, x_rstd n0, probs b3, ctx n0, probs b4, x2_bias c0, probs b5, o b0, probs b6, "
            "o b1, probs b7, o b2, probs n0, o b3, residual b0, probs n1")
        GPSIMD_END = in_order(
            "x2_rstd c0, probs b2, probs b3, x2_bias c0, probs b4, o b0, probs b5, probs b6, o b1, probs b7, "
            "o b2, o b3, residual b0, x2_rstd b0, x2_bias b0")
        FREES = {"q": q_lo, "k": k_lo, "v": v_lo, "xT": xT_lo, "wo": x2_ready, "x2T": x2T_lo, "gateT": gateT_ready,
                 "gate": down_ready, "downT": downT_ready, "up": inter_lo, "y": y_ready}
        bank_of = {(what, k): i % 2 for i, (what, _, k) in
                   enumerate(u for u in TENSOR_ORDER if u[0] in FREES)}

        def bank(what, k):
            return g_ps[bank_of[what, k]][:, :]

        def as_two(ps):
            return ps.rearrange("p (a n) -> p a n", a=2)

        def parts(t, table):
            return [(what, {"b": t, "c": t - 1, "n": t + 1}[who], k) for what, who, k in table]

        def wait_bank(pe, so_far, what, k):
            before = [u for u in so_far if bank_of.get((u[0], u[2])) == bank_of[what, k]]
            if before:
                what, s, k = before[-1]
                wait(pe, FREES[what], s, k)

        gate_buf = den_T[:, 0:KC * GA].rearrange("p (k n) -> p k n", k=KC)
        lora_buf = [x2[:, :, :].rearrange("p i d -> p (i d)"), x2n[:, :, :].rearrange("p i d -> p (i d)")]

        def rows_piece(w, src, k, buf):
            return src[128 * k:128 * k + 128, :], buf[:, :], [part[:, k, :] for part in w]

        def chunks_piece(w, src, i, buf):
            n = w[0].shape[1] // 2
            return (src.rearrange("(c p) n -> p c n", p=128)[:, n * i:n * i + n, :],
                    buf[:, :].rearrange("p (c n) -> p c n", c=n), [part[:, n * i:n * i + n, :] for part in w])

        PIECES = ([rows_piece(wq, Wq, i, w_buf[i]) for i in range(2)]
                  + [rows_piece(wk, Wkv[:, 0:INNER], i, w_buf[2 + i]) for i in range(2)]
                  + [rows_piece(wv, Wkv[:, INNER:2 * INNER], i, w_buf[4 + i]) for i in range(2)]
                  + [chunks_piece(wo, Wo, i, w_buf[6 + i]) for i in range(2)]
                  + [(gateA.rearrange("(k p) n -> p k n", p=128), gate_buf,
                      [part[:, :, :] for part in gate_w])]
                  + [rows_piece(wi, wiT, i, w_buf[i]) for i in range(2)]
                  + [(None, lora_buf[i], [lora_w[:, 512 * i:512 * i + 512]]) for i in range(2)]
                  + [chunks_piece(wf, woT, i, w_buf[2 + i]) for i in range(2)])
        WQ, WK, WV, WO, GATE, WI, LORA, WF = 1, 3, 5, 7, 8, 10, 12, 14

        block = ctx.enter_context(nc.Block())

        @block.sync
        def _(sp):
            def load_x(b):
                wait(sp, xT_mm, b, -1)
                sp.dma_start(x_in[:, :, :], x[bass.ds(b, 1), :, :].rearrange("a (i p) d -> p (a i) d", p=128)) \
                    .then_inc(x_loaded, 16)

            def load_ctx(b):
                wait(sp, ctx_lo, b, -1)
                sp.dma_start(c_in[:, :, :], ctxT[bass.ds(b, 1), :, :, :].rearrange("a p k m -> p (a k) m")) \
                    .then_inc(ctx_loaded, 16)

            def load_residual(b):
                wait(sp, y_ready, b, -1)
                sp.dma_start(x2[:, :, :], x[bass.ds(b, 1), :, :].rearrange("a (i p) d -> p (a i) d", p=128)) \
                    .then_inc(res_loaded, 16)

            def store(b):
                wait(sp, y_ready, b, IT - 1)
                sp.dma_start(out[bass.ds(b, 1), :, :].rearrange("a (i p) d -> p (a i) d", p=128), x2n[:, :, :]) \
                    .then_inc(y_stored, 16)

            def load(n):
                src, buf, _ = PIECES[n]
                sp.dma_start(buf, src).then_inc(w_loaded[n], 16)

            def small(buf, src):
                sp.dma_start(buf, src).then_inc(small_loaded, 16)

            load_x(0)
            load(0)
            load(1)
            load_ctx(0)
            for n in range(WK - 1, WV + 1):
                load(n)
            small(gates[:, 0:1], g_xattn[0:1, :].to_broadcast([128, 1]))
            small(gates[:, 1:2], g_ffn[0:1, :].to_broadcast([128, 1]))
            small(mask_u8[:, :], mask)
            small(bo_row[:, :], bo[0:1, :].to_broadcast([128, D]))
            small(fb_row[:, :], wo_b[0:1, :].to_broadcast([128, D]))
            small(gb_row[:, :], gate_b[0:1, :].to_broadcast([128, E]))
            load(GATE)
            load(WO - 1)
            load(WO)
            load_x(1)
            load_ctx(1)
            sp.wait_ge(pool_const, 2)
            for n in range(2):
                buf, cols = lora_buf[n], slice(512 * n, 512 * n + 512)
                for q in range(3):
                    sp.dma_start(buf[ER * q:ER * q + ER, :], loraB[:, cols]).then_inc(w_loaded[LORA - 1 + n], 16)
                sp.dma_start(buf[96:98, :], wi_b[0:1, cols].to_broadcast([2, 512])) \
                    .then_inc(w_loaded[LORA - 1 + n], 16)
            sp.wait_ge(w_lo, WQ + 1)
            load(WI - 1)
            load(WI)
            sp.wait_ge(w_lo, WK + 1)
            load(WF - 1)
            load(WF)
            sp.wait_ge(w_lo, LORA + 1)
            load_residual(0)

            def iteration(t):
                load_x(t + 1)
                load_ctx(t + 1)
                store(t - 1)
                load_residual(t)

            iteration(1)
            with sp.Fori(2, B - 1) as t:
                iteration(t)
            store(B - 2)
            load_residual(B - 1)
            store(B - 1)
            wait(sp, y_stored, B - 1)

        @block.gpsimd
        def _(pool):
            pool.memset(ident[:, :], 0.0).then_inc(ident_zero, 1)
            pool.wait_ge(ident_zero, 1)
            pool.affine_select(out=ident[:, :], in_=ident[:, :], compare_op=ALU.not_equal, fill=1.0,
                               base=0, pattern=[[-1, 128]], channel_multiplier=1).then_inc(ident_ready, 1)
            pool.wait_ge(ident_ready, 1)
            pool.memset(x2[96:128, :, :], 0.0).then_inc(pool_const, 1)
            pool.memset(x2n[96:128, :, :], 0.0).then_inc(pool_const, 1)
            pool.wait_ge(pool_const, 2)
            pool.memset(lo_rows[:, :], 0.0).then_inc(pool_const, 1)
            pool.memset(neg_half[:, :], -0.5).then_inc(pool_const, 1)
            for e in range(E):
                last = pool.memset(rank[:, :, e:e + 1], float(E - e))
            last.then_inc(pool_const, 1)
            pool.wait_ge(pool_const, 5)
            pool.memset(lo_rows[2 * ER:3 * ER, :], -1.0).then_inc(pool_const, 1)
            pool.wait_ge(pool_const, 6)
            pool.affine_select(out=lo_rows[:, :], in_=lo_rows[:, :], compare_op=ALU.not_equal, fill=-1.0,
                               base=-97, pattern=[[0, 1]], channel_multiplier=1).then_inc(pool_const, 1)

            def rstd_of(out_, var, ready, done, b):
                wait(pool, ready, b)
                pool.tensor_tensor(out_[:, :], var[:, :], neg_half[:, :], ALU.pow).then_inc(done, 1)

            def split_o(b, g):
                wait(pool, wo_mm, b, -1)
                wait(pool, o_hi, b, g)
                if isinstance(b, int) and b == 0:
                    pool.wait_ge(w_lo, WO + 1)
                s = 2 * (g % 2)
                pool.tensor_tensor(oT[1][:, 2 * g:2 * g + 2, :], o_raw[:, s:s + 2, :],
                                   as_f32(oT[0][:, 2 * g:2 * g + 2, :]), ALU.subtract).then_inc(o_lo, 1)

            def iteration(t, table):
                for what, s, k in parts(t, table):
                    if what == "o":
                        split_o(s, k)
                    elif what == "ctx":
                        wait(pool, ctx_hi, s)
                        pool.tensor_tensor(cT[1][:, :, :], c_in[:, :, :], as_f32(cT[0][:, :, :]), ALU.subtract) \
                            .then_inc(ctx_lo, 1)
                    elif what == "ones":
                        pool.wait_ge(pool_const, 7)
                        wait(pool, rstd_ready, s)
                        pool.memset(as_f32(down_s[:, :, 96:98]), 1.0)
                        pool.memset(as_f32(down_s[:, :, 98:128]), 0.0)
                        pool.memset(as_f32(v[0][:, :, :, 1, :]), 1.0)
                        pool.memset(as_f32(v[1][:, :, :, 1, :]), 0.0).then_inc(ones_set, 1)
                    elif what == "probs":
                        wait(pool, probs_hi, s, k)
                        hi, lo = [part[:, k % 2, 1, :, :] for part in probs]
                        pool.tensor_tensor(lo, exp_s[:, k % 2, 1, :, :], as_f32(hi), ALU.subtract) \
                            .then_inc(probs2_lo, 1)
                    elif what == "residual":
                        wait(pool, res_loaded, s)
                        if isinstance(s, int) and s == 0:
                            pool.wait_ge(biases_scaled, 1)
                        pool.tensor_tensor(x2[:, :, :], x2[:, :, :], bo_row[:, None, :].to_broadcast([128, IT, D]),
                                           ALU.add).then_inc(res_biased, 1)
                    elif what == "x_rstd":
                        rstd_of(rstd, var_eps, var_ready, rstd_ready, s)
                    elif what == "x2_rstd":
                        rstd_of(rstd2, var_eps2, var2_ready, rstd2_ready, s)
                    elif what == "x2_bias":
                        wait(pool, x2_normed, s)
                        pool.tensor_tensor(x2[:, :, :], x2[:, :, :], fb_row[:, None, :].to_broadcast([128, IT, D]),
                                           ALU.add).then_inc(x2_biased, 1)

            iteration(0, GPSIMD_START)
            iteration(1, GPSIMD_ORDER)
            with pool.Fori(2, B - 1) as t:
                iteration(t, GPSIMD_ORDER)
            iteration(B - 1, GPSIMD_END)

        @block.scalar
        def _(act):
            def evac(out_, in_, done, func=ACT.Copy):
                act.activation(out_, in_, func).then_inc(done, 1)

            def exps(b, p):
                wait(act, s_mm, b, p)
                wait(act, pv_mm, b, p - 2)
                act.activation(exp_s[:, p % 2, :, :, :], s_ps[p % 2][:, :, :, :], ACT.Exp, scale=SCALE) \
                    .then_inc(exp_done, 1)

            def copy_den(b, p):
                wait(act, pv_mm, b, p)
                wait(act, o_lo, b, p // 2 - 2)
                slot = p % 4
                act.activation(o_raw[0:64, slot, :], o_ps[p % 2][64:128, 0, :], ACT.Copy)
                act.activation(o_raw[64:128, slot, :], o_ps[p % 2][0:64, 1, :], ACT.Copy).then_inc(den_copied, 1)

            def split_o(b, g):
                wait(act, wo_mm, b, -1)
                if isinstance(b, int) and b == 0:
                    act.wait_ge(w_lo, WO + 1)
                wait(act, o_normed, b, 2 * g + 1)
                s = 2 * (g % 2)
                evac(oT[0][:, 2 * g:2 * g + 2, :], o_raw[:, s:s + 2, :], o_hi)

            def part(what, s, k):
                src = bank(what, k) if what in FREES else None
                if what == "w":
                    split_piece(k)
                elif what == "tanh":
                    act.wait_ge(small_loaded, 16 * 6)
                    act.activation(tgate[:, :], gates[:, :], ACT.Tanh).then_inc(tanh_done, 1)
                elif what == "exp":
                    exps(s, k)
                elif what == "probs":
                    wait(act, clipped, s, k)
                    evac(probs[0][:, k % 2, :, :, :], exp_s[:, k % 2, :, :, :], probs_hi)
                elif what == "den":
                    copy_den(s, k)
                elif what == "o":
                    split_o(s, k)
                elif what == "ctx":
                    split_ctx(s)
                elif what == "q":
                    wait(act, q_mm, s, k)
                    wait(act, s_mm, s, 2 * k - 3)
                    two = as_two(src)
                    act.activation(q_parts[0:64, k % 2, :, 0, :], two[0:64], ACT.Copy)
                    evac(q_parts[64:128, k % 2, :, 1, :], two[64:128], q_hi)
                elif what == "k":
                    wait(act, k_mm, s, k)
                    wait(act, s_mm, s, 2 * k - 3)
                    two = as_two(src)
                    act.activation(k_twice[0:64, k % 2, :, 0, :], two[0:64], ACT.Copy)
                    evac(k_twice[64:128, k % 2, :, 1, :], two[64:128], k_hi)
                elif what == "k_twice":
                    slot = k_twice[:, k % 2, :, :, :]
                    wait(act, k_hi, s, k)
                    act.activation(slot[64:128, :, 0, :], as_f32(slot[0:64, :, 0, :]), ACT.Copy)
                    evac(slot[0:64, :, 1, :], as_f32(slot[64:128, :, 1, :]), k_doubled)
                elif what == "v":
                    half, j = divmod(k, 2)
                    wait(act, v_mm, s, k)
                    wait(act, pv_mm, s, NP // 2 * (half + 1) - 1 - NP)
                    evac(v[0][:, j, 4 * half:4 * half + 4, 0:3:2, :],
                         src.rearrange("p (a b d) -> p a b d", b=2, d=DH), v_hi)
                elif what == "xT":
                    wait(act, xT_mm, s)
                    wait(act, q_mm, s, -1)
                    evac(xT[0][:, :, :], src.rearrange("p (k t) -> p k t", k=KC), xT_hi)
                elif what == "x2T":
                    wait(act, x2T_mm, s)
                    evac(x2T[0][:, :, :], src.rearrange("p (k t) -> p k t", k=KC), x2T_hi)
                elif what == "gateT":
                    wait(act, gateT_mm, s)
                    evac(gateT, src[0:GA, 0:T], gateT_ready)
                elif what == "downT":
                    wait(act, downT_mm, s)
                    evac(downT[:, :], src[:, 0:T], downT_ready)
                elif what == "up":
                    wait(act, up_mm, s, k)
                    wait(act, y_mm, s, -1)
                    if isinstance(s, int) and s == 0:
                        act.wait_ge(w_lo, WF + 1)
                    evac(inter[0][:, 2 * k:2 * k + 2, :], src.rearrange("p (f t) -> p f t", f=2), inter_hi, ACT.Relu)

            def split_ctx(b):
                wait(act, ctx_loaded, b)
                wait(act, k_mm, b, -1)
                wait(act, v_mm, b, -1)
                evac(cT[0][:, :, :], c_in[:, :, :], ctx_hi)

            def split_piece(n):
                _, buf, w = PIECES[n]
                act.wait_ge(w_loaded[n], 16 * 4 if n in (LORA - 1, LORA) else 16)
                evac(w[0], buf, w_hi)

            def iteration(t, table):
                for what, s, k in parts(t, table):
                    part(what, s, k)

            iteration(0, SCALAR_START)
            iteration(1, SCALAR_ORDER)
            with act.Fori(2, B - 1) as t:
                iteration(t, SCALAR_ORDER)
            iteration(B - 1, SCALAR_END)

        @block.tensor
        def _(pe):
            def three(out_, lhs, rhs, cut_l, cut_r, start, stop):
                pe.matmul(out_, cut_l(lhs[0]), cut_r(rhs[0]), start=start, stop=False)
                pe.matmul(out_, cut_l(lhs[0]), cut_r(rhs[1]), start=False, stop=False)
                return pe.matmul(out_, cut_l(lhs[1]), cut_r(rhs[0]), start=False, stop=stop)

            def scores(b, p):
                wait(pe, exp_done, b, p - 2)
                wait(pe, q_lo, b, p // 2)
                wait(pe, k_lo, b, p // 2)
                wait(pe, k_doubled, b, p // 2)
                slot, a = p // 2 % 2, p % 2
                ps = s_ps[p % 2]
                for j in range(JC):
                    keys = slice(128 * j, 128 * j + 128)
                    for h in range(2):
                        pe.matmul(ps[:, h, j, :], k_twice[:, slot, a, h, keys], q_parts[:, slot, a, h, :],
                                  start=True, stop=False)
                    for h, rows in enumerate(HEAD_ROWS):
                        last = pe.matmul(ps[:, h, j, :], kT_lo[rows, slot, a, keys], q_parts[rows, slot, a, h, :],
                                         start=False, stop=True)
                last.then_inc(s_mm, 1)

            def apply(b, p):
                wait(pe, probs_lo, b, p)
                wait(pe, probs2_lo, b, p)
                wait(pe, o_normed, b, p - 2)
                wait(pe, v_lo, b, 1 + 2 * (p // (NP // 2)))
                if isinstance(b, int) and b == 0 and p == 0:
                    pe.wait_ge(ones_set, 1)
                for h in range(2):
                    for j in range(JC):
                        last = three(o_ps[p % 2][:, h, :], v, probs,
                                     lambda w: w[:, j, p, h:h + 2, :].rearrange("k a d -> k (a d)"),
                                     lambda w: w[:, p % 2, h, j, :], j == 0, j == JC - 1)
                last.then_inc(pv_mm, 1)

            def unit(so_far, what, s, k):
                ps = bank(what, k)
                wait_bank(pe, so_far, what, k)
                if what == "q":
                    wait(pe, xT_lo, s)
                    if isinstance(s, int) and s == 0:
                        pe.wait_ge(w_lo, WQ + 1)
                    for a in range(2):
                        cols = slice(128 * (2 * k + a), 128 * (2 * k + a) + 128)
                        for c in range(KC):
                            last = three(ps[:, T * a:T * a + T], wq, xT, lambda w: w[:, c, cols],
                                         lambda w: w[:, c, :], c == 0, c == KC - 1)
                    last.then_inc(q_mm, 1)
                elif what == "k":
                    wait(pe, ctx_lo, s)
                    if isinstance(s, int) and s == 0:
                        pe.wait_ge(w_lo, WK + 1)
                    for a in range(2):
                        cols = slice(128 * (2 * k + a), 128 * (2 * k + a) + 128)
                        for c in range(KC):
                            last = three(ps[:, M * a:M * a + M], wk, cT, lambda w: w[:, c, cols],
                                         lambda w: w[:, c, :], c == 0, c == KC - 1)
                    last.then_inc(k_mm, 1)
                elif what == "v":
                    half, j = divmod(k, 2)
                    wait(pe, ctx_lo, s)
                    if isinstance(s, int) and s == 0:
                        pe.wait_ge(w_lo, WV + 1)
                    for c in range(KC):
                        last = three(ps[:, :], cT, wv, lambda w: w[:, c, 128 * j:128 * j + 128],
                                     lambda w: w[:, c, 512 * half:512 * half + 512], c == 0, c == KC - 1)
                    last.then_inc(v_mm, 1)
                elif what == "xT":
                    wait(pe, x_normed, s)
                    for c in range(KC):
                        for i in range(IT):
                            last = pe.transpose(ps[:, T * c + 128 * i:T * c + 128 * i + 128],
                                                x_in[:, i, 128 * c:128 * c + 128], ident[:, :])
                    last.then_inc(xT_mm, 1)
                elif what == "wo":
                    wait(pe, o_lo, s, NG - 1)
                    if isinstance(s, int) and s == 0:
                        pe.wait_ge(w_lo, WO + 1)
                    for c in range(NP):
                        last = three(ps[:, 0:D], oT, wo, lambda w: w[:, c, 128 * k:128 * k + 128],
                                     lambda w: w[:, c, :], c == 0, c == NP - 1)
                    last.then_inc(wo_mm, 1)
                elif what == "x2T":
                    wait(pe, x2_normed, s)
                    for c in range(KC):
                        for i in range(IT):
                            last = pe.transpose(ps[:, T * c + 128 * i:T * c + 128 * i + 128],
                                                x2n[:, i, 128 * c:128 * c + 128], ident[:, :])
                    last.then_inc(x2T_mm, 1)
                elif what == "gateT":
                    wait(pe, x2T_lo, s)
                    if isinstance(s, int) and s == 0:
                        pe.wait_ge(w_lo, GATE + 1)
                    for c in range(KC):
                        last = three(ps[0:GA, 0:T], gate_w, x2T, lambda w: w[:, c, :], lambda w: w[:, c, :],
                                     c == 0, c == KC - 1)
                    last.then_inc(gateT_mm, 1)
                elif what == "gate":
                    wait(pe, gateT_ready, s)
                    for i in range(IT):
                        last = pe.matmul(ps[:, 64 * i:64 * i + GA], gateT[:, 128 * i:128 * i + 128],
                                         ident[0:GA, 0:GA], start=True, stop=True)
                    last.then_inc(gate_mm, 1)
                elif what == "downT":
                    wait(pe, down_ready, s)
                    for i in range(IT):
                        last = pe.transpose(ps[:, 128 * i:128 * i + 128], as_f32(down_s[:, i, :]), ident[:, :])
                    last.then_inc(downT_mm, 1)
                elif what == "up":
                    wait(pe, x2T_lo, s)
                    if isinstance(s, int) and s == 0:
                        pe.wait_ge(w_lo, LORA + 1)
                    for a in range(2):
                        cols = slice(128 * (2 * k + a), 128 * (2 * k + a) + 128)
                        o = ps[:, T * a:T * a + T]
                        for c in range(KC):
                            three(o, wi, x2T, lambda w: w[:, c, cols], lambda w: w[:, c, :], c == 0, False)
                        wait(pe, downT_ready, s)
                        last = pe.matmul(o, lora_w[:, cols], downT[:, :], start=False, stop=True)
                    last.then_inc(up_mm, 1)
                elif what == "y":
                    wait(pe, inter_lo, s, 3)
                    if isinstance(s, int) and s == 0:
                        pe.wait_ge(w_lo, WF + 1)
                    for f in range(FC):
                        last = three(ps[:, 0:D], inter, wf, lambda w: w[:, f, 128 * k:128 * k + 128],
                                     lambda w: w[:, f, :], f == 0, f == FC - 1)
                    last.then_inc(y_mm, 1)

            def iteration(t, table, before):
                done = before
                for what, s, k in parts(t, table):
                    if what == "scores":
                        scores(s, k)
                    elif what == "apply":
                        apply(s, k)
                    else:
                        unit(done, what, s, k)
                    done = done + [(what, s, k)]

            pe.wait_ge(ident_ready, 1)
            iteration(0, TENSOR_START, [])
            iteration(1, TENSOR_ORDER, parts(0, TENSOR_START))
            with pe.Fori(2, B - 1) as t:
                iteration(t, TENSOR_ORDER, parts(t - 1, TENSOR_ORDER))
            iteration(B - 1, TENSOR_END, parts(B - 2, TENSOR_ORDER))

        @block.vector
        def _(dve):
            def sub(out_, in_, hi, done):
                dve.tensor_tensor(out_, in_, as_f32(hi), ALU.subtract).then_inc(done, 1)

            def clip(b, p):
                wait(dve, exp_done, b, p)
                wait(dve, bound_set, b)
                for j in range(JC):
                    e = exp_s[:, p % 2, :, j, :]
                    last = dve.tensor_scalar(e, e, bound_b[:, j:j + 1], LO_BOUND, ALU.min, ALU.max)
                last.then_inc(clipped, 1)

            def norm_o(b, p):
                slot = p % 4
                wait(dve, den_copied, b, p)
                if isinstance(b, int) and b == 0 and p == 0:
                    dve.wait_ge(w_lo, GATE + 1)
                dve.transpose(den_T[:, :], o_raw[:, slot, :]).then_inc(den_turned, 1)
                wait(dve, den_turned, b, p)
                dve.reciprocal(den_inv[:, :], den_T[:, 0:T:32]).then_inc(inverted, 1)
                wait(dve, inverted, b, p)
                dve.transpose(o_raw[:, slot, :].rearrange("p (a b) -> p a b", b=32),
                              den_inv[:, :, None].to_broadcast([128, T // 32, 32])).then_inc(inv_spread, 1)
                wait(dve, inv_spread, b, p)
                dve.tensor_tensor(o_raw[0:64, slot, :], o_ps[p % 2][0:64, 0, :], o_raw[0:64, slot, :], ALU.mult)
                dve.tensor_tensor(o_raw[64:128, slot, :], o_ps[p % 2][64:128, 1, :], o_raw[64:128, slot, :],
                                  ALU.mult).then_inc(o_normed, 1)

            def layer_stats(src, st, mo, ve, done, mdone, ready, b):
                for i in range(IT):
                    dve.bn_stats(st[:, i, :], src[:, i, :]).then_inc(done, 1)
                wait(dve, done, b, IT - 1)
                dve.tensor_copy(ve[:, 0:1], st[:, IT - 1, 0:1])
                for i in range(IT):
                    dve.bn_aggr(mo[:, i, :], st[:, i, :]).then_inc(mdone, 1)
                wait(dve, mdone, b, IT - 1)
                dve.tensor_scalar(ve[:, :], mo[:, :, 1], EPS, None, ALU.add).then_inc(ready, 1)

            def normalise(dst, src, mo, rs, ready, done, b):
                wait(dve, ready, b)
                for i in range(IT):
                    last = dve.tensor_scalar(dst[:, i, :], src[:, i, :], mo[:, i, 0:1], rs[:, i:i + 1],
                                             ALU.subtract, ALU.mult)
                last.then_inc(done, 1)

            FROM = {"choose": "gate", "x2": "wo"}

            def choose(b, ps):
                g = ps[:, 0:128].rearrange("p (i n) -> p i n", i=IT)
                wait(dve, gate_mm, b)
                dve.tensor_tensor(logits[:, :, :], g[:, :, 0:E], gb_row[:, None, :].to_broadcast([128, IT, E]),
                                  ALU.add).then_inc(pick, 1)
                wait(dve, pick, b, 0)
                dve.tensor_reduce(top[:, :], logits[:, :, :], AX.X, ALU.max).then_inc(pick, 1)
                wait(dve, pick, b, 1)
                dve.tensor_tensor(ranked[:, :, :], logits[:, :, :], top[:, :, None].to_broadcast([128, IT, E]),
                                  ALU.is_equal).then_inc(pick, 1)
                wait(dve, pick, b, 2)
                dve.tensor_tensor(ranked[:, :, :], ranked[:, :, :], rank[:, :, :], ALU.mult).then_inc(pick, 1)
                wait(dve, pick, b, 3)
                dve.tensor_reduce(first[:, :], ranked[:, :, :], AX.X, ALU.max).then_inc(pick, 1)
                wait(dve, pick, b, 4)
                dve.tensor_tensor(chosen[:, :, :], ranked[:, :, :], first[:, :, None].to_broadcast([128, IT, E]),
                                  ALU.is_equal).then_inc(pick, 1)
                wait(dve, pick, b, 5)
                for i in range(IT):
                    last = dve.tensor_tensor(down[:, i, :].rearrange("p (e r) -> p e r", r=R),
                                             g[:, i, E:GA].rearrange("p (e r) -> p e r", r=R),
                                             chosen[:, i, :, None].to_broadcast([128, E, R]), ALU.mult)
                last.then_inc(pick, 1)
                wait(dve, pick, b, 6)
                wait(dve, downT_mm, b, -1)
                dve.tensor_copy(down_s[:, :, 2 * ER:3 * ER], down[:, :, :])
                dve.tensor_copy(down_s[:, :, 0:ER], down[:, :, :]).then_inc(pick, 1)
                wait(dve, pick, b, 7)
                sub(down_s[:, :, ER:2 * ER], down[:, :, :], down_s[:, :, 0:ER], down_ready)

            def part(what, s, k):
                src = bank(FROM.get(what, what), k) if FROM.get(what, what) in FREES else None
                two = as_two(src) if src is not None else None
                if what == "w":
                    split_piece(k)
                elif what == "biases":
                    dve.wait_ge(tanh_done, 1)
                    dve.tensor_scalar(bo_row[:, :], bo_row[:, :], tgate[:, 0:1], None, ALU.mult)
                    dve.tensor_scalar(fb_row[:, :], fb_row[:, :], tgate[:, 1:2], None, ALU.mult) \
                        .then_inc(biases_scaled, 1)
                elif what == "bounds":
                    dve.wait_ge(small_loaded, 16 * 6)
                    dve.tensor_scalar(bound[:, :], mask_u8[:, :], HI_BOUND - LO_BOUND, LO_BOUND, ALU.mult, ALU.add) \
                        .then_inc(bounds_set, 1)
                elif what == "clip":
                    if k == 0:
                        if isinstance(s, int) and s == 0:
                            dve.wait_ge(bounds_set, 1)
                        wait(dve, clipped, s, -1)
                        dve.tensor_copy(bound_b[:, :], bound[:, bass.ds(s * JC, JC)]).then_inc(bound_set, 1)
                    clip(s, k)
                elif what == "probs":
                    wait(dve, probs_hi, s, k)
                    sub(probs[1][:, k % 2, 0, :, :], exp_s[:, k % 2, 0, :, :], probs[0][:, k % 2, 0, :, :], probs_lo)
                elif what == "norm":
                    norm_o(s, k)
                elif what == "x_stats":
                    wait(dve, x_loaded, s)
                    layer_stats(x_in, stats, moments, var_eps, stats_done, moments_done, var_ready, s)
                elif what == "x2_stats":
                    wait(dve, x2_ready, s, IT - 1)
                    layer_stats(x2, stats2, moments2, var_eps2, stats2_done, moments2_done, var2_ready, s)
                elif what == "x_norm":
                    normalise(x_in, x_in, moments, rstd, rstd_ready, x_normed, s)
                elif what == "x2_norm":
                    wait(dve, y_stored, s, -1)
                    normalise(x2n, x2, moments2, rstd2, rstd2_ready, x2_normed, s)
                elif what == "v":
                    half, j = divmod(k, 2)
                    wait(dve, v_hi, s, k)
                    cols = slice(4 * half, 4 * half + 4)
                    sub(v[1][:, j, cols, 0:3:2, :], src.rearrange("p (a b d) -> p a b d", b=2, d=DH),
                        v[0][:, j, cols, 0:3:2, :], v_lo)
                elif what == "q":
                    wait(dve, q_hi, s, k)
                    slot = q_parts[:, k % 2, :, :, :]
                    dve.tensor_tensor(slot[64:128, :, 0, :], two[0:64], as_f32(slot[0:64, :, 0, :]), ALU.subtract)
                    sub(slot[0:64, :, 1, :], two[64:128], slot[64:128, :, 1, :], q_lo)
                elif what == "k":
                    wait(dve, k_hi, s, k)
                    hi, lo = k_twice[:, k % 2, :, :, :], kT_lo[:, k % 2, :, :]
                    dve.tensor_tensor(lo[0:64], two[0:64], as_f32(hi[0:64, :, 0, :]), ALU.subtract)
                    sub(lo[64:128], two[64:128], hi[64:128, :, 1, :], k_lo)
                elif what == "xT":
                    wait(dve, xT_hi, s)
                    sub(xT[1][:, :, :], two, xT[0][:, :, :], xT_lo)
                elif what == "x2":
                    wait(dve, wo_mm, s, k)
                    wait(dve, res_biased, s)
                    dve.scalar_tensor_tensor(x2[:, k, :], src[:, 0:D], tgate[:, 0:1], x2[:, k, :],
                                             ALU.mult, ALU.add).then_inc(x2_ready, 1)
                elif what == "x2T":
                    wait(dve, x2T_hi, s)
                    sub(x2T[1][:, :, :], two, x2T[0][:, :, :], x2T_lo)
                elif what == "choose":
                    choose(s, src)
                elif what == "up":
                    wait(dve, inter_hi, s, k)
                    dve.scalar_tensor_tensor(inter[1][:, 2 * k:2 * k + 2, :], two, 0.0,
                                             as_f32(inter[0][:, 2 * k:2 * k + 2, :]), ALU.max,
                                             ALU.subtract).then_inc(inter_lo, 1)
                elif what == "y":
                    wait(dve, y_mm, s, k)
                    wait(dve, x2_biased, s)
                    dve.scalar_tensor_tensor(x2n[:, k, :], src[:, 0:D], tgate[:, 1:2], x2[:, k, :],
                                             ALU.mult, ALU.add).then_inc(y_ready, 1)

            def split_piece(n):
                _, buf, w = PIECES[n]
                dve.wait_ge(w_hi, n + 1)
                if n in (LORA - 1, LORA):
                    dve.wait_ge(pool_const, 7)
                    dve.scalar_tensor_tensor(w[0], as_f32(w[0]), lo_rows[:, 0:1], buf, ALU.mult, ALU.add) \
                        .then_inc(w_lo, 1)
                else:
                    sub(w[1], buf, w[0], w_lo)

            def iteration(t, table):
                for what, s, k in parts(t, table):
                    part(what, s, k)

            iteration(0, VECTOR_START)
            iteration(1, VECTOR_ORDER)
            with dve.Fori(2, B - 1) as t:
                iteration(t, VECTOR_ORDER)
            iteration(B - 1, VECTOR_END)


def kernel(**inputs):
    import numpy as _np
    import concourse.bacc as _bacc
    from concourse import mybir as _mybir
    from concourse.bass_utils import run_bass_kernel_spmd as _run

    a = {k: _np.asarray(v) for k, v in inputs.items()}
    B, M, D = a["ctx_1024"].shape
    E, R, _ = a["L0_ffn_lora_A"].shape
    F = a["L0_ffn_wi_W"].shape[0]
    feeds = {
        "x": a["x"],
        "ctxT": a["ctx_1024"].reshape(B, M, D // 128, 128).transpose(0, 3, 2, 1),
        "mask": a["mask_BxS2_bk1"].reshape(B, M // 128, 128).transpose(2, 0, 1).reshape(128, -1),
        "g_xattn": a["g_xattn"].reshape(1, 1),
        "g_ffn": a["g_ffn"].reshape(1, 1),
        "Wq": a["L0_xattn_Wq"],
        "Wkv": a["L0_xattn_Wkv"],
        "Wo": a["L0_xattn_Wo"],
        "bo": a["L0_xattn_bo"].reshape(1, -1),
        "gateA": _np.concatenate([a["L0_ffn_gate_W"].T, a["L0_ffn_lora_A"].reshape(E * R, D).T], axis=1),
        "gate_b": a["L0_ffn_gate_b"].reshape(1, -1),
        "wiT": a["L0_ffn_wi_W"].T,
        "wi_b": a["L0_ffn_wi_b"].reshape(1, -1),
        "woT": a["L0_ffn_wo_W"].T,
        "wo_b": a["L0_ffn_wo_b"].reshape(1, -1),
        "loraB": a["L0_ffn_lora_B"].transpose(0, 2, 1).reshape(E * R, F),
    }
    nc = _bacc.Bacc("TRN2", target_bir_lowering=False, num_devices=1, dynamic_dma_scratch_size=512)
    arrays, args = {}, []
    for name, value in feeds.items():
        value = _np.ascontiguousarray(value)
        arrays[f"in_{name}"] = value
        args.append(nc.dram_tensor(f"in_{name}", value.shape, _mybir.dt.from_np(value.dtype),
                                   kind="ExternalInput").ap())
    out = nc.dram_tensor("out_y", a["x"].shape, _mybir.dt.float32, kind="ExternalOutput").ap()
    gated_cross_attention_and_lora_ffn(nc, *args, out)
    r = _run(nc, [arrays], core_ids=[0])
    return r.results[0]["out_y"]
```
